# Optimizing a Trainium2 kernel written in Bass

```python
import numpy as np
import jax
import jax.numpy as jnp

def _softmax(x, axis=-1):
    return jax.nn.softmax(x, axis=axis)

def _gelu(x):
    return jax.nn.gelu(x, approximate=True)

def _silu(x):
    return jax.nn.silu(x)

def _sigmoid(x):
    return jax.nn.sigmoid(x)

def _layernorm(x, axis=-1, eps=1e-05):
    m = jnp.mean(x, axis=axis, keepdims=True)
    v = jnp.var(x, axis=axis, keepdims=True)
    return (x - m) / jnp.sqrt(v + eps)

def _scatter_add(tgt, idx, src, axis=0):
    return tgt.at[idx].add(src)

def _segment_sum(src, seg, n):
    return jax.ops.segment_sum(src, seg, n)
kernel_name = 'mk_adj_ffn_d1_adj_r2_a80c9a'

def setup_inputs(seed: int=0):
    np.random.seed(seed)
    _w = jnp.asarray

    def _rec_inputs():
        import jax
        import jax.numpy as jnp
        _gk = jax.random.key(seed)
        x = 7.22e-05 + 1 * jax.random.normal(jax.random.fold_in(_gk, 1), (128, 128, 128), jnp.float32)
        _a = jax.random.bernoulli(jax.random.fold_in(_gk, 2), 0.125, (128, 128, 128))
        _a = jnp.logical_or(_a, jnp.swapaxes(_a, -1, -2))
        _a = jnp.logical_or(_a, jnp.eye(128, dtype=bool))
        adj = _a.astype(jnp.int32)
        return (x, adj)
    x, adj = _rec_inputs()

    def _L0_gnn_setup():
        import jax, jax.numpy as jnp
        import numpy as np
        B, S, D = (64, 256, 128)

        def _leaky(x):
            return jnp.where(x >= 0, x, 0.2 * x)
        key = jax.random.key(seed)
        k = jax.random.split(key, 6)
        stdv = 1.0 / np.sqrt(D)
        return {'hidden': jax.random.normal(k[0], (B, S, D), dtype=jnp.float32), 'adj': jax.random.randint(k[1], (B, S, S), 0, 5, dtype=jnp.int32), 'a0': jax.random.uniform(k[2], (D, 1), jnp.float32, -stdv, stdv), 'a1': jax.random.uniform(k[3], (D, 1), jnp.float32, -stdv, stdv), 'a2': jax.random.uniform(k[4], (D, 1), jnp.float32, -stdv, stdv), 'a3': jax.random.uniform(k[5], (D, 1), jnp.float32, -stdv, stdv), 'bias': jnp.zeros((D,), dtype=jnp.float32)}
    _L0_gnn_all = _L0_gnn_setup()
    _L0_gnn_in = {k: v for k, v in _L0_gnn_all.items() if k in ('a0', 'a1', 'a2', 'a3', 'bias')}
    del _L0_gnn_all

    def _L0_ffn_setup():
        import jax, jax.numpy as jnp
        import numpy as np
        D_MODEL = 128
        N_EXPERTS = 16
        HIDDEN = 256
        SCALE = 0.02
        key = jax.random.key(seed)
        ks = jax.random.split(key, 5)
        x = jax.random.normal(ks[0], (4, 4096, D_MODEL), dtype=jnp.float32)
        gate_w = jax.random.normal(ks[1], (D_MODEL, N_EXPERTS), dtype=jnp.float32) * SCALE
        gate_b = jnp.zeros((N_EXPERTS,), dtype=jnp.float32)
        w1 = jax.random.normal(ks[2], (N_EXPERTS, D_MODEL, HIDDEN), dtype=jnp.float32) * SCALE
        w2 = jax.random.normal(ks[3], (N_EXPERTS, D_MODEL, HIDDEN), dtype=jnp.float32) * SCALE
        w3 = jax.random.normal(ks[4], (N_EXPERTS, HIDDEN, D_MODEL), dtype=jnp.float32) * SCALE
        return {'x': x, 'gate_w': gate_w, 'gate_b': gate_b, 'w1': w1, 'w2': w2, 'w3': w3}
    _L0_ffn_all = _L0_ffn_setup()
    _L0_ffn_in = {k: v for k, v in _L0_ffn_all.items() if k in ('gate_w', 'gate_b', 'w1', 'w2', 'w3')}
    del _L0_ffn_all
    return {'x': x, 'adj': adj, 'L0_gnn_a0': _L0_gnn_in['a0'], 'L0_gnn_a1': _L0_gnn_in['a1'], 'L0_gnn_a2': _L0_gnn_in['a2'], 'L0_gnn_a3': _L0_gnn_in['a3'], 'L0_gnn_bias': _L0_gnn_in['bias'], 'L0_ffn_gate_w': _L0_ffn_in['gate_w'], 'L0_ffn_gate_b': _L0_ffn_in['gate_b'], 'L0_ffn_w1': _L0_ffn_in['w1'], 'L0_ffn_w2': _L0_ffn_in['w2'], 'L0_ffn_w3': _L0_ffn_in['w3']}

def reference(x, adj, L0_gnn_a0, L0_gnn_a1, L0_gnn_a2, L0_gnn_a3, L0_gnn_bias, L0_ffn_gate_w, L0_ffn_gate_b, L0_ffn_w1, L0_ffn_w2, L0_ffn_w3):
    import jax
    import jax.numpy as jnp

    def _L0_gnn_ref(hidden, adj, a0, a1, a2, a3, bias):
        import jax, jax.numpy as jnp
        import numpy as np
        B, S, D = (64, 256, 128)

        def _leaky(x):
            return jnp.where(x >= 0, x, 0.2 * x)
        h = hidden

        def e_of(a):
            return _leaky(jnp.einsum('bid,bjd->bij', h * a[:, 0], h))
        e0, e1, e2, e3 = (e_of(a0), e_of(a1), e_of(a2), e_of(a3))
        neg_inf = jnp.float32(-jnp.finfo(e0.dtype).max)
        alpha = jnp.where(adj == 1, e0, neg_inf)
        alpha = jnp.where(adj == 2, e1, alpha)
        alpha = jnp.where(adj == 3, e2, alpha)
        alpha = jnp.where(adj == 4, e3, alpha)
        alpha = jax.nn.sigmoid(alpha)
        return jnp.einsum('bij,bjd->bid', alpha, h) + bias

    def _L0_ffn_ref(x, gate_w, gate_b, w1, w2, w3):
        import jax, jax.numpy as jnp
        import numpy as np
        D_MODEL = 128
        N_EXPERTS = 16
        HIDDEN = 256
        SCALE = 0.02
        n_experts = w1.shape[0]
        logits = jnp.einsum('bsd,de->bse', x, gate_w) + gate_b
        probs = jax.nn.softmax(logits, axis=-1)
        top_probs, top_idx = jax.lax.top_k(probs, 2)
        top_probs = top_probs / jnp.sum(top_probs, axis=-1, keepdims=True)
        dispatch = jnp.sum(jax.nn.one_hot(top_idx, n_experts, dtype=x.dtype) * top_probs[..., None], axis=-2)
        h1 = jnp.einsum('bsd,edh->bseh', x, w1)
        h2 = jnp.einsum('bsd,edh->bseh', x, w2)
        hidden = jax.nn.silu(h1) * h2
        expert_out = jnp.einsum('bseh,eho->bseo', hidden, w3)
        return jnp.einsum('bseo,bse->bso', expert_out, dispatch)
    x = x + _L0_gnn_ref(_layernorm(x, axis=-1), adj, L0_gnn_a0, L0_gnn_a1, L0_gnn_a2, L0_gnn_a3, L0_gnn_bias)
    x = x + _L0_ffn_ref(_layernorm(x, axis=-1), L0_ffn_gate_w, L0_ffn_gate_b, L0_ffn_w1, L0_ffn_w2, L0_ffn_w3)
    return x

_drawn_inputs = setup_inputs


def setup_inputs(seed=0):
    import zlib

    import numpy as np

    out = dict(_drawn_inputs(seed))
    spreads = {'L0_gnn_bias': (0.0, 0.272), 'L0_ffn_gate_b': (0.0, 0.8)}
    factors = {'L0_ffn_gate_w': 8.0, 'L0_ffn_w1': 8.0, 'L0_ffn_w2': 8.0, 'L0_ffn_w3': 8.0}
    for name, (base, spread) in spreads.items():
        noise = np.random.default_rng([zlib.crc32(name.encode()), seed]).standard_normal(out[name].shape)
        drawn = base * np.exp(spread * noise) if base else spread * noise
        out[name] = jnp.asarray(drawn.astype(out[name].dtype))
    for name, factor in factors.items():
        out[name] = (out[name] * factor).astype(out[name].dtype)
    return out
```

```python
from contextlib import ExitStack

import concourse.bass as bass
from concourse import mybir

G, P, D = 128, 128, 128
E, HID = 16, 256
KINDS = 4
GB = 4
GROUPS = G // GB
EPS = 1e-5
NEG = -1.0e30
TOKENS = G * P
CAP = TOKENS + P
FULL_TILES = 2 * TOKENS // P
TILES = FULL_TILES + E - 1
DUMMY = E * CAP
XS_ROWS = DUMMY + E * P
Y_ROWS = 2 * TOKENS + 2 * E * P
ROW = D + 2
TPG = FULL_TILES // GROUPS
LAG = 4
RING = 16
YRING = 8
NEW = TPG + E - 1
LAST = TILES - (TPG * (GROUPS - 1) - (E - 1))
LIST = TILES + LAST
DEPTH = 4

ALU = mybir.AluOpType
ACT = mybir.ActivationFunctionType
F32 = mybir.dt.float32
BF16 = mybir.dt.bfloat16
U16 = mybir.dt.uint16
U32 = mybir.dt.uint32
I32 = mybir.dt.int32
X = mybir.AxisListType.X


def build(nc, x, adj, a0, a1, a2, a3, bias, gate_w, gate_b, w1, w2, w3, out):
    xs = nc.dram_tensor("dispatched", [XS_ROWS, ROW], F32, kind="Internal").ap()
    y = nc.dram_tensor("expert_rows", [Y_ROWS, D], F32, kind="Internal").ap()

    with ExitStack() as ctx:
        def sb(name, shape, dt=F32):
            return ctx.enter_context(nc.sbuf_tensor(name, shape, dt))

        def ps(name):
            return ctx.enter_context(nc.psum_tensor(name, [P, 512], F32))

        def sem(name):
            return ctx.enter_context(nc.semaphore(name))

        xall = sb("xall", [P, G * D])
        w12 = sb("w12", [P, E * 2 * HID])
        w3s = sb("w3s", [P, E * 2 * D])
        adji = [sb(f"adji{b}", [P, GB * P], I32) for b in range(2)]
        adjb = sb("adjb", [P, GB * P], BF16)
        st = sb("st", [P, 2 * GB, 6])
        mv = sb("mv", [P, 2 * GB, 2])
        ve = sb("ve", [P, 2 * GB])
        rs = sb("rs", [P, 2 * GB])
        nt = sb("nt", [P, 2 * GB])
        hN = sb("hN", [P, GB * D])
        hT = sb("hT", [P, GB * P])
        sc = sb("sc", [P, GB, KINDS, P])
        adjT = sb("adjT", [P, GB * P], BF16)
        mask = sb("mask", [P, KINDS, GB * P], U16)
        sel = sb("sel", [P, GB * P])
        lk = sb("lk", [P, GB * P])
        al = sb("al", [P, GB * P])
        hx = [sb(f"hx{b}", [P, 2 * GB * ROW]) for b in range(2)]
        h2T = sb("h2T", [P, GB * P])
        lg = sb("lg", [P, GB, E])
        lg2 = sb("lg2", [P, GB, E])
        eq = sb("eq", [P, GB, E])
        wq = sb("wq", [P, GB, E])
        oh1 = sb("oh1", [P, GB, E])
        oh2 = sb("oh2", [P, GB, E])
        m1 = sb("m1", [P, GB])
        m2 = sb("m2", [P, GB])
        mx = sb("mx", [P, GB])
        dlt = sb("dlt", [P, GB])
        th = sb("th", [P, GB])
        dsp = sb("dsp", [P, GB * E], BF16)
        pos = sb("pos", [P, GB, E])
        pm = sb("pm", [P, 2, GB, E])
        slotf = sb("slotf", [P, 2, GB])
        slot = [sb(f"slot{b}", [P, 2 * GB], U32) for b in range(2)]
        run = sb("run", [P, E])
        tok = sb("tok", [P, GROUPS * 2 * GB], I32)
        xg = [sb(f"xg{r}", [P, ROW]) for r in range(RING)]
        xh = [sb(f"xh{b}", [P, 3 * P]) for b in range(2)]
        sl = [sb(f"sl{b}", [P, HID]) for b in range(2)]
        hid = [sb(f"hid{b}", [P, HID]) for b in range(2)]
        yo = [sb(f"yo{r}", [P, D]) for r in range(YRING)]
        padx = sb("padx", [P, E, ROW])
        padi = sb("padi", [P, E], I32)
        padi2 = sb("padi2", [P, E], I32)
        pslot = sb("pslot", [P, E], U32)
        basef = sb("basef", [1, E])
        cnti = sb("cnti", [1, E], I32)
        cnth = sb("cnth", [1, E], I32)
        full = sb("full", [1, E])
        done = sb("done", [1, E])
        new = sb("new", [1, E])
        pre = [sb(f"pre{i}", [1, 2 * E]) for i in range(2)]
        sx = sb("sx", [1, E])
        reg = sb("reg", [1, E + 1])
        dreg = sb("dreg", [1, E])
        cmp = sb("cmp", [1, LAST, E])
        pr = sb("pr", [1, LAST, E])
        ek = sb("ek", [1, LAST])
        rr = sb("rr", [1, LAST])
        cidx = sb("cidx", [1, LAST])
        cidx128 = sb("cidx128", [1, LAST])
        listE = sb("listE", [1, LIST], I32)
        listR = sb("listR", [1, LIST], I32)
        tailf = sb("tailf", [1, 1])
        taili = sb("taili", [1, 1], I32)
        ident = sb("ident", [P, P])
        identb = sb("identb", [P, P], BF16)
        tri = sb("tri", [P, P], BF16)
        ones = sb("ones", [P, P], BF16)
        acol = sb("acol", [P, KINDS])
        biasr = sb("biasr", [P, D])
        gw = sb("gw", [P, E])
        gbr = sb("gbr", [P, E])
        wt = sb("wt", [P, E])
        iop = sb("iop", [P, 1])

        bE = ctx.enter_context(nc.psum_tensor("bE", [P, 2, 512], F32))
        bT, bR, bH0, bH1, bXH, bO = [ps(n) for n in ("bT", "bR", "bH0", "bH1", "bXH", "bO")]
        bH = [bH0, bH1]
        adjTp = bR[:, 0:GB * P // 2].bitcast(BF16)

        s_x = [sem(f"x_landed{b}") for b in range(2)]
        s_adj = [sem(f"adj_landed{b}") for b in range(2)]
        s_w = sem("weights_landed")
        s_small = sem("small_landed")
        s_c = sem("pool_constants")
        s_cv = sem("dve_constants")
        s_pad0 = sem("pads_built")
        s_dummy = sem("dummy_tiles_stored")
        s_ln = sem("norm_steps")
        s_h = sem("h_written")
        s_adjb = sem("adj_cast")
        s_th = sem("h_transposed")
        s_sc = sem("h_scaled")
        s_adjT = sem("adjT_copied")
        s_mask = sem("masks")
        s_clr = sem("sel_cleared")
        s_e = sem("e_ready")
        s_sel = sem("e_selected")
        s_lk = sem("leaky")
        s_tanh = sem("tanh")
        s_al = sem("alpha")
        s_go = sem("gnn_out")
        s_xb = sem("x_plus_bias")
        s_x1 = sem("x1_written")
        s_h2 = sem("h2_written")
        s_t2 = sem("h2_transposed")
        s_h2T = sem("h2T_copied")
        s_lg = sem("logits")
        s_rt = sem("route_steps")
        s_gt = sem("gate_tanh")
        s_gate = sem("gates_written")
        s_pf = sem("prefix")
        s_so = sem("slot_steps")
        s_li = sem("list_steps")
        s_list = sem("list_appended")
        s_disp = [sem(f"dispatched{b}") for b in range(2)]
        s_padi = sem("pad_slots")
        s_pads = sem("pads_stored")
        s_xg = [sem(f"tile_landed{r}") for r in range(RING)]
        s_tp = sem("tile_transposed")
        s_xh = sem("tile_transposes_copied")
        s_hp = sem("h_products")
        s_sl = sem("silu")
        s_hid = sem("hidden")
        s_o = sem("expert_out")
        s_yo = sem("expert_out_gated")
        s_y = [sem(f"rows_stored{r}") for r in range(YRING)]
        s_apart = sem("waits_taken_apart")
        s_yin = [sem(f"y_loaded{r}") for r in range(4)]
        s_a1 = sem("first_sum")
        s_a2 = sem("second_sum")
        s_out = [sem(f"out_stored{r}") for r in range(4)]

        block = ctx.enter_context(nc.Block())

        def wait(eng, s, count):
            if not isinstance(count, int) or count > 0:
                eng.wait_ge(s, count)

        def apart(eng):
            eng.sem_inc(s_apart, 1)

        def bc(ap, shape):
            return ap.to_broadcast(shape)

        ORDER = ["ADJ", "F0", "T1", "LOG", "F1", "ROUTE", "MASK", "F2", "E01", "PREF", "F3", "SLOT", "E23",
                 "F4", "D0", "TANH", "F5", "D1", "LIST", "OUT", "F6", "LN2", "F7", "T2"]
        BEHIND = {"LOG", "ROUTE", "PREF", "SLOT", "LIST", "D0", "D1"}
        LAST_S = (TILES - 1 + DEPTH + TPG * LAG) // (2 * TPG)

        def walk(fn, s, first, last):
            for b in range(2):
                for step in ORDER:
                    if step[0] == "F":
                        c = TPG * (b - LAG) + int(step[1:])
                        if 2 * TPG * last + c >= 0 and 2 * TPG * first + c < TILES + DEPTH:
                            fn("F", s, b, c)
                        continue
                    lo, hi = 2 * first + b, 2 * last + b
                    if step in BEHIND:
                        if hi >= 1 and lo <= GROUPS:
                            fn(step, s if b else s - 1, 1 - b, None)
                    elif lo < GROUPS:
                        fn(step, s, b, None)

        LOOP = (3, GROUPS // 2 - 1)

        def program(eng, fn):
            for s in range(LOOP[0]):
                walk(fn, s, s, s)
            with eng.Fori(LOOP[0], LOOP[1]) as s:
                walk(fn, s, LOOP[0], LOOP[1] - 1)
            for s in range(LOOP[1], LAST_S + 1):
                walk(fn, s, s, s)

        def has(s, c):
            return not isinstance(s, int) or 0 <= 2 * TPG * s + c < TILES

        def tile(s, c):
            return s * (2 * TPG) + c

        def lap(s, c, ring):
            per = 2 * TPG // ring
            return s * per + (c // ring) + 1

        hxv = [h[:, :].rearrange("p (c g r) -> p c g r", c=2, r=ROW) for h in hx]

        @block.sync
        def _(sp):
            x_g = x.rearrange("g p d -> p g d")
            adj_g = adj.rearrange("g i j -> i g j")

            def load_group(u, s, b):
                if isinstance(u, int) and u >= GROUPS:
                    return
                sp.dma_start(xall[:, bass.ds(u * (GB * D), GB * D)].rearrange("p (g d) -> p g d", g=GB),
                             x_g[:, bass.ds(u * GB, GB), :]).then_inc(s_x[b], 16)
                sp.dma_start(adji[b][:, :].rearrange("p (g d) -> p g d", g=GB),
                             adj_g[:, bass.ds(u * GB, GB), :]).then_inc(s_adj[b], 16)

            load_group(0, 0, 0)
            sp.dma_start(acol[:, 0:1], a0).then_inc(s_small, 16)
            sp.dma_start(acol[:, 1:2], a1).then_inc(s_small, 16)
            sp.dma_start(acol[:, 2:3], a2).then_inc(s_small, 16)
            sp.dma_start(acol[:, 3:4], a3).then_inc(s_small, 16)
            sp.dma_start(biasr[:, :], bias.rearrange("(a d) -> a d", a=1).to_broadcast([P, D])).then_inc(s_small, 16)
            sp.dma_start(gbr[:, :], gate_b.rearrange("(a d) -> a d", a=1).to_broadcast([P, E])).then_inc(s_small, 16)
            sp.dma_start(gw[:, :], gate_w).then_inc(s_small, 16)
            load_group(1, 0, 1)
            w12v = w12[:, :].rearrange("p (e w h) -> p e w h", e=E, w=2)
            sp.dma_start(w12v[:, :, 0, :], w1.rearrange("e d h -> d e h")).then_inc(s_w, 16)
            sp.dma_start(w12v[:, :, 1, :], w2.rearrange("e d h -> d e h")).then_inc(s_w, 16)
            sp.dma_start(w3s[:, :].rearrange("p (e c o) -> p e c o", e=E, c=2),
                         w3.rearrange("e (c p) o -> p e c o", c=2)).then_inc(s_w, 16)
            sp.wait_ge(s_pad0, 1)
            sp.dma_start(xs[DUMMY:DUMMY + E * P, :].rearrange("(e p) r -> p e r", p=P), padx[:, :, :]).then_inc(s_dummy, 16)
            sp.wait_ge(s_dummy, 16)

            def body(step, s, b, c):
                u = s * 2 + b
                if step == "T1" and not (isinstance(s, int) and u + 2 >= GROUPS):
                    wait(sp, s_adjb, u + 1)
                    apart(sp)
                    load_group(u + 2, s + 1, b)
                if step == "F" and has(s, c):
                    if (c + TPG * LAG) % TPG == 0:
                        if not (isinstance(s, int) and u - 1 > GROUPS):
                            wait(sp, s_list, u - 1)
                            apart(sp)
                            wait(sp, s_disp[b], s * (2 * GB * 16))
                        if isinstance(s, int) and u == GROUPS + 1:
                            sp.wait_ge(s_pads, 16 * E)
                    row = sp.value_load(listR[0:1, bass.ds(tile(s, c), 1)], min_val=0, max_val=XS_ROWS - P)
                    wait(sp, s_y[c % YRING], 16 * lap(s, c - RING, YRING))
                    sp.dma_start(xg[c % RING][:, :], xs[bass.ds(row, P), :]).then_inc(s_xg[c % RING], 16)

            program(sp, body)

            yin = [w12[:, r * 1024:(r + 1) * 1024] for r in range(4)]
            y_g = y[0:2 * TOKENS, :].rearrange("(g p c) d -> p g (c d)", p=P, c=2)
            for r in range(YRING):
                last = max(t for t in range(TILES) if t % YRING == r)
                sp.wait_ge(s_y[r], 16 * (last // YRING + 1))
            sp.wait_ge(s_hp, TILES)
            for r in range(4):
                sp.dma_start(yin[r].rearrange("p (g d) -> p g d", g=GB), y_g[:, r * GB:(r + 1) * GB, :]).then_inc(s_yin[r], 16)
            with sp.Fori(1, GROUPS // 4) as t:
                for r in range(4):
                    sp.wait_ge(s_a2, t * 4 + (r - 3))
                    sp.dma_start(yin[r].rearrange("p (g d) -> p g d", g=GB),
                                 y_g[:, bass.ds(t * (4 * GB) + r * GB, GB), :]).then_inc(s_yin[r], 16)

        @block.gpsimd
        def _(pool):
            nc.gpsimd.memset(ident[:, :], 0.0).then_inc(s_c, 1)
            nc.gpsimd.memset(identb[:, :], 0.0).then_inc(s_c, 1)
            nc.gpsimd.memset(tri[:, :], 1.0).then_inc(s_c, 1)
            nc.gpsimd.memset(ones[:, :], 1.0).then_inc(s_c, 1)
            nc.gpsimd.memset(padx[:, :, :], 0.0).then_inc(s_c, 1)
            nc.gpsimd.iota(wt[:, :], pattern=[[-1, E]], base=E, channel_multiplier=0,
                           allow_small_or_imprecise_dtypes=True).then_inc(s_c, 1)
            nc.gpsimd.iota(iop[:, :], pattern=[[0, 1]], base=0, channel_multiplier=1,
                           allow_small_or_imprecise_dtypes=True).then_inc(s_c, 1)
            nc.gpsimd.iota(run[:, :], pattern=[[CAP, E]], base=0, channel_multiplier=0,
                           allow_small_or_imprecise_dtypes=True).then_inc(s_c, 1)
            nc.gpsimd.iota(basef[:, :], pattern=[[CAP, E]], base=0, channel_multiplier=0,
                           allow_small_or_imprecise_dtypes=True).then_inc(s_c, 1)
            nc.gpsimd.iota(cidx[:, :], pattern=[[1, LAST]], base=0, channel_multiplier=0,
                           allow_small_or_imprecise_dtypes=True).then_inc(s_c, 1)
            nc.gpsimd.iota(cidx128[:, :], pattern=[[P, LAST]], base=0, channel_multiplier=0,
                           allow_small_or_imprecise_dtypes=True).then_inc(s_c, 1)
            nc.gpsimd.iota(tok[:, :].rearrange("p (u c g) -> p u c g", c=2, g=GB),
                           pattern=[[2 * P * GB, GROUPS], [1, 2], [2 * P, GB]], base=0, channel_multiplier=2).then_inc(s_c, 1)
            nc.gpsimd.iota(padi[:, :], pattern=[[P, E]], base=2 * TOKENS, channel_multiplier=1).then_inc(s_c, 1)
            nc.gpsimd.iota(padi2[:, :], pattern=[[P, E]], base=2 * TOKENS + E * P, channel_multiplier=1).then_inc(s_c, 1)
            pool.wait_ge(s_c, 14)
            nc.gpsimd.affine_select(out=ident[:, :], in_=ident[:, :], compare_op=ALU.not_equal, fill=1.0,
                                    base=0, pattern=[[-1, P]], channel_multiplier=1).then_inc(s_c, 1)
            nc.gpsimd.affine_select(out=identb[:, :], in_=identb[:, :], compare_op=ALU.not_equal, fill=1.0,
                                    base=0, pattern=[[-1, P]], channel_multiplier=1).then_inc(s_c, 1)
            nc.gpsimd.affine_select(out=tri[:, :], in_=tri[:, :], compare_op=ALU.is_gt, fill=0.0,
                                    base=0, pattern=[[1, P]], channel_multiplier=-1).then_inc(s_c, 1)

            def dispatch(s, b, half):
                u = s * 2 + b
                if half == 0:
                    pool.wait_ge(s_so, u * 6 + 6)
                    pool.wait_ge(s_gate, u + 1)
                    apart(pool)
                for n in range(half * GB, half * GB + GB):
                    nc.gpsimd.indirect_dma_start(
                        out=xs[:, :], out_offset=bass.IndirectOffsetOnAxis(ap=slot[b][:, n:n + 1], axis=0),
                        in_=hx[b][:, n * ROW:(n + 1) * ROW], in_offset=None).then_inc(s_disp[b], 16)

            def body(step, s, b, c):
                u = s * 2 + b
                if step == "ADJ":
                    wait(pool, s_lk, u)
                    apart(pool)
                    nc.gpsimd.memset(sel[:, :], NEG).then_inc(s_clr, 1)
                if step == "D0":
                    dispatch(s, b, 0)
                if step == "D1":
                    dispatch(s, b, 1)
                if step == "LIST" and isinstance(s, int) and u == GROUPS - 1:
                    pool.wait_ge(s_padi, 2)
                    for e in range(E):
                        nc.gpsimd.indirect_dma_start(
                            out=xs[:, :], out_offset=bass.IndirectOffsetOnAxis(ap=pslot[:, e:e + 1], axis=0),
                            in_=padx[:, e, :], in_offset=None).then_inc(s_pads, 16)
                if step == "F" and has(s, c - DEPTH):
                    o = c - DEPTH
                    wait(pool, s_yo, tile(s, o) + 1)
                    apart(pool)
                    nc.gpsimd.indirect_dma_start(
                        out=y[:, :],
                        out_offset=bass.IndirectOffsetOnAxis(ap=xg[o % RING][:, D:D + 1].bitcast(U32), axis=0),
                        in_=yo[o % YRING][:, :], in_offset=None).then_inc(s_y[o % YRING], 16)

            program(pool, body)

        @block.tensor
        def _(pe):
            pe.wait_ge(s_c, 17)
            pe.wait_ge(s_small, 16 * 7)

            def body(step, s, b, c):
                u = s * 2 + b
                if step == "T1":
                    wait(pe, s_h, u + 1)
                    wait(pe, s_h2T, u)
                    for g in range(GB):
                        last = nc.tensor.transpose(bT[:, g * P:(g + 1) * P], hN[:, g * D:(g + 1) * D], ident[:, :])
                    last.then_inc(s_th, 1)
                    wait(pe, s_adjb, u + 1)
                    wait(pe, s_so, u * 6 - 6)
                    for g in range(GB):
                        last = nc.tensor.transpose(adjTp[:, g * P:(g + 1) * P], adjb[:, g * P:(g + 1) * P], identb[:, :])
                    last.then_inc(s_th, 1)
                if step in ("E01", "E23"):
                    wait(pe, s_sc, u + 1)
                    pair = 0 if step == "E01" else 1
                    wait(pe, s_sel, (u * 2 + pair) * KINDS)
                    for g in (2 * pair, 2 * pair + 1):
                        nc.tensor.matmul(bE[:, g % 2, :], hT[:, g * P:(g + 1) * P], sc[:, g, :, :].rearrange("p k i -> p (k i)"),
                                         start=True, stop=True).then_inc(s_e, 1)
                if step == "OUT":
                    wait(pe, s_al, u + 1)
                    for g in range(GB):
                        last = nc.tensor.matmul(bT[:, g * D:(g + 1) * D], al[:, g * P:(g + 1) * P], hN[:, g * D:(g + 1) * D],
                                                start=True, stop=True)
                    last.then_inc(s_go, 1)
                if step == "T2":
                    wait(pe, s_h2, u + 1)
                    for g in range(GB):
                        last = nc.tensor.transpose(bT[:, g * P:(g + 1) * P], hxv[b][:, 0, g, 0:D], ident[:, :])
                    last.then_inc(s_t2, 1)
                if step == "LOG":
                    wait(pe, s_h2T, u + 1)
                    wait(pe, s_adjT, (u + 2) if not (isinstance(s, int) and u + 1 >= GROUPS) else GROUPS)
                    for g in range(GB):
                        last = nc.tensor.matmul(bR[:, g * E:(g + 1) * E], h2T[:, g * P:(g + 1) * P], gw[:, :], start=True, stop=True)
                    last.then_inc(s_lg, 1)
                if step == "PREF":
                    wait(pe, s_rt, u * 14 + 13)
                    n = GB * E
                    nc.tensor.matmul(bR[:, n:2 * n], tri[:, :], dsp[:, :], start=True, stop=False, skip_group_check=True)
                    for g in range(1, GB):
                        nc.tensor.matmul(bR[:, n + g * E:2 * n], ones[:, :], dsp[:, 0:n - g * E], start=False, stop=(g == GB - 1),
                                         skip_group_check=True)
                    for g in range(GB):
                        last = nc.tensor.matmul(bR[:, 2 * n:2 * n + E], ones[:, :], dsp[:, g * E:(g + 1) * E],
                                                start=False, stop=(g == GB - 1), skip_group_check=True)
                    last.then_inc(s_pf, 1)
                if step == "F":
                    slot_f(s, b, c)

            def slot_f(s, b, c):
                u = s * 2 + b
                x_, h_, t_, o_ = c, c - 1, c - 3, c - DEPTH
                if isinstance(s, int) and tile(s, c) == 0:
                    pe.wait_ge(s_w, 48)
                if has(s, x_) or has(s, t_):
                    if (c + TPG * LAG) % TPG == 0 and not (isinstance(s, int) and u - 1 > GROUPS):
                        wait(pe, s_list, u - 1)
                    wait(pe, s_xh, tile(s, c))
                    last = None
                    if has(s, x_):
                        wait(pe, s_xg[x_ % RING], 16 * lap(s, x_, RING))
                        last = nc.tensor.transpose(bXH[:, 0:P], xg[x_ % RING][:, 0:D], ident[:, :])
                    if has(s, t_):
                        wait(pe, s_hid, tile(s, t_) + 1)
                        for h in range(2):
                            last = nc.tensor.transpose(bXH[:, (1 + h) * P:(2 + h) * P], hid[t_ % 2][:, h * P:(h + 1) * P], ident[:, :])
                    last.then_inc(s_tp, 1)
                if has(s, h_):
                    e = pe.value_load(listE[0:1, bass.ds(tile(s, h_), 1)], min_val=0, max_val=E - 1)
                    wait(pe, s_xh, tile(s, h_) + 1)
                    wait(pe, s_hid, tile(s, h_) - 1)
                    nc.tensor.matmul(bH[h_ % 2][:, :], xh[h_ % 2][:, 0:P], w12[:, bass.ds(e * (2 * HID), 2 * HID)],
                                     start=True, stop=True).then_inc(s_hp, 1)
                if has(s, o_):
                    e = pe.value_load(listE[0:1, bass.ds(tile(s, o_), 1)], min_val=0, max_val=E - 1)
                    wait(pe, s_xh, tile(s, c))
                    wait(pe, s_yo, tile(s, o_))
                    for h in range(2):
                        last = nc.tensor.matmul(bO[:, 0:D], xh[(c - 1) % 2][:, (1 + h) * P:(2 + h) * P],
                                                w3s[:, bass.ds(e * (2 * D) + h * D, D)], start=(h == 0), stop=(h == 1))
                    last.then_inc(s_o, 1)

            program(pe, body)

        @block.scalar
        def _(act):
            act.wait_ge(s_small, 16 * 7)

            def body(step, s, b, c):
                u = s * 2 + b
                if step == "T1":
                    wait(act, s_th, u * 2 + 1)
                    wait(act, s_e, u * GB)
                    for k in range(KINDS):
                        nc.scalar.activation(sc[:, :, k, :], bT[:, :].rearrange("p (g i) -> p g i", g=GB), ACT.Copy,
                                             scale=acol[:, k:k + 1])
                    nc.scalar.activation(hT[:, :], bT[:, :], ACT.Copy).then_inc(s_sc, 1)
                    wait(act, s_th, u * 2 + 2)
                    wait(act, s_mask, u)
                    nc.scalar.activation(adjT[:, :], adjTp[:, :], ACT.Copy).then_inc(s_adjT, 1)
                if step == "ROUTE":
                    wait(act, s_rt, u * 14 + 14)
                    wait(act, s_gate, u)
                    nc.scalar.activation(th[:, :], dlt[:, :], ACT.Tanh, scale=0.5).then_inc(s_gt, 1)
                if step == "TANH":
                    wait(act, s_lk, u + 1)
                    wait(act, s_go, u)
                    nc.scalar.activation(al[:, :], lk[:, :], ACT.Tanh, scale=0.5).then_inc(s_tanh, 1)
                if step == "T2":
                    wait(act, s_t2, u + 1)
                    wait(act, s_lg, u)
                    nc.scalar.activation(h2T[:, :], bT[:, :], ACT.Copy).then_inc(s_h2T, 1)
                if step == "F":
                    x_, h_, t_, o_ = c, c - 1, c - 3, c - DEPTH
                    if has(s, x_) or has(s, t_):
                        lo = 0 if has(s, x_) else P
                        hi = 3 * P if has(s, t_) else P
                        wait(act, s_tp, tile(s, c) + 1)
                        wait(act, s_hp, tile(s, c) - 1 if has(s, c - 2) else 0)
                        wait(act, s_o, tile(s, c) - 4)
                        nc.scalar.activation(xh[c % 2][:, lo:hi], bXH[:, lo:hi], ACT.Copy).then_inc(s_xh, 1)
                    if has(s, h_):
                        wait(act, s_hp, tile(s, h_) + 1)
                        wait(act, s_hid, tile(s, h_) - 1)
                        nc.scalar.activation(sl[h_ % 2][:, :], bH[h_ % 2][:, 0:HID], ACT.Silu).then_inc(s_sl, 1)
                    if has(s, o_):
                        wait(act, s_o, tile(s, o_) + 1)
                        wait(act, s_y[o_ % YRING], 16 * (lap(s, o_, YRING) - 1))
                        nc.scalar.activation(yo[o_ % YRING][:, :], bO[:, 0:D], ACT.Copy,
                                             scale=xg[o_ % RING][:, D + 1:D + 2]).then_inc(s_yo, 1)

            program(act, body)

            yout = [w3s[:, r * 512:(r + 1) * 512] for r in range(4)]
            out_g = out.rearrange("g p d -> p g d")
            with act.Fori(0, GROUPS // 4) as t:
                for r in range(4):
                    act.wait_ge(s_a2, t * 4 + (r + 1))
                    act.dma_start(out_g[:, bass.ds(t * (4 * GB) + r * GB, GB), :],
                                  yout[r].rearrange("p (g d) -> p g d", g=GB)).then_inc(s_out[r], 16)
            for r in range(4):
                act.wait_ge(s_out[r], 16 * (GROUPS // 4))

        @block.vector
        def _(dve):
            v = nc.vector
            LI = 17
            dve.wait_ge(s_c, 17)
            dve.wait_ge(s_small, 16 * 7)
            v.memset(done[:, :], 0.0)
            v.memset(pre[0][:, :], 0.0)
            v.memset(pre[1][:, :], 0.0)
            v.memset(tailf[:, :], 0.0)
            v.memset(taili[:, :], 0).then_inc(s_cv, 1)
            v.tensor_copy(padx[:, :, D:D + 1].bitcast(U32), padi[:, :]).then_inc(s_pad0, 1)
            dve.wait_ge(s_cv, 1)

            NORM = 13

            def norm(at, lo, hi, src):
                apart(dve)
                for g in range(lo, hi):
                    last = v.bn_stats(st[:, g, :], src(g))
                last.then_inc(s_ln, 1)
                dve.wait_ge(s_ln, at + 1)
                apart(dve)
                for g in range(lo, hi):
                    last = v.bn_aggr(mv[:, g, :], st[:, g, :])
                last.then_inc(s_ln, 1)
                dve.wait_ge(s_ln, at + 2)
                V, R, T = ve[:, lo:hi], rs[:, lo:hi], nt[:, lo:hi]
                v.tensor_single_scalar(V, mv[:, lo:hi, 1], EPS, ALU.add).then_inc(s_ln, 1)
                dve.wait_ge(s_ln, at + 3)
                v.tensor_scalar(R.bitcast(I32), V.bitcast(I32), -0.5, 1597463007.0, ALU.mult, ALU.add).then_inc(s_ln, 1)
                dve.wait_ge(s_ln, at + 4)
                for i in range(3):
                    v.scalar_tensor_tensor(T, R, -0.5, R, ALU.mult, ALU.mult).then_inc(s_ln, 1)
                    dve.wait_ge(s_ln, at + 5 + 3 * i)
                    v.tensor_tensor(T, T, V, ALU.mult).then_inc(s_ln, 1)
                    dve.wait_ge(s_ln, at + 6 + 3 * i)
                    v.scalar_tensor_tensor(R, T, 1.5, R, ALU.add, ALU.mult).then_inc(s_ln, 1)
                    dve.wait_ge(s_ln, at + 7 + 3 * i)

            def apply(into, src, g, n):
                return v.tensor_scalar(into, src, mv[:, n, 0:1], rs[:, n:n + 1], ALU.subtract, ALU.mult)

            def rows(u, g):
                return xall[:, bass.ds(u * (GB * D) + g * D, D)]

            def first_norm(u):
                wait(dve, s_go, u)
                for g in range(GB):
                    last = apply(hN[:, g * D:(g + 1) * D], rows(u, g), g, GB + g)
                last.then_inc(s_h, 1)
                dve.wait_ge(s_h, u + 1)
                xu = xall[:, bass.ds(u * (GB * D), GB * D)].rearrange("p (g d) -> p g d", g=GB)
                v.tensor_tensor(xu, xu, bc(biasr[:, None, :], [P, GB, D]), ALU.add).then_inc(s_xb, 1)

            def one_hot_of_max(src, m, oh, base):
                v.tensor_reduce(m[:, :], src[:, :, :], X, ALU.max).then_inc(s_rt, 1)
                dve.wait_ge(s_rt, base + 1)
                v.tensor_tensor(eq[:, :, :], src[:, :, :], bc(m[:, :, None], [P, GB, E]), ALU.is_equal).then_inc(s_rt, 1)
                dve.wait_ge(s_rt, base + 2)
                v.tensor_tensor(wq[:, :, :], eq[:, :, :], bc(wt[:, None, :], [P, GB, E]), ALU.mult).then_inc(s_rt, 1)
                dve.wait_ge(s_rt, base + 3)
                v.tensor_reduce(mx[:, :], wq[:, :, :], X, ALU.max).then_inc(s_rt, 1)
                dve.wait_ge(s_rt, base + 4)
                v.tensor_tensor(oh[:, :, :], wq[:, :, :], bc(mx[:, :, None], [P, GB, E]), ALU.is_equal).then_inc(s_rt, 1)
                dve.wait_ge(s_rt, base + 5)

            def append(u, final):
                n = LAST if final else NEW
                at = u * LI
                v.tensor_tensor(cnti[:, :], run[0:1, :], basef[:, :], ALU.subtract).then_inc(s_li, 1)
                dve.wait_ge(s_li, at + 1)
                if final:
                    v.tensor_single_scalar(cnti[:, :], cnti[:, :], P - 1, ALU.add).then_inc(s_cv, 1)
                    dve.wait_ge(s_cv, 2)
                v.tensor_single_scalar(cnth[:, :], cnti[:, :], 7, ALU.arith_shift_right).then_inc(s_li, 1)
                dve.wait_ge(s_li, at + 2)
                v.tensor_copy(full[:, :], cnth[:, :]).then_inc(s_li, 1)
                dve.wait_ge(s_li, at + 3)
                v.tensor_tensor(pre[0][:, E:2 * E], full[:, :], done[:, :], ALU.subtract).then_inc(s_li, 1)
                dve.wait_ge(s_li, at + 4)
                v.tensor_copy(new[:, :], pre[0][:, E:2 * E])
                for i in range(4):
                    d = 1 << i
                    v.tensor_tensor(pre[1 - i % 2][:, E:2 * E], pre[i % 2][:, E:2 * E], pre[i % 2][:, E - d:2 * E - d],
                                    ALU.add).then_inc(s_li, 1)
                    dve.wait_ge(s_li, at + 5 + i)
                S = pre[0][:, E:2 * E]
                v.tensor_tensor(sx[:, :], new[:, :], S, ALU.subtract).then_inc(s_li, 1)
                dve.wait_ge(s_li, at + 9)
                v.tensor_tensor(sx[:, :], sx[:, :], done[:, :], ALU.add).then_inc(s_li, 1)
                v.tensor_tensor(cmp[:, 0:n, :], bc(cidx[:, 0:n, None], [1, n, E]), bc(S[:, None, :], [1, n, E]), ALU.is_ge)
                dve.wait_ge(s_li, at + 10)
                v.scalar_tensor_tensor(reg[:, 0:E], sx[:, :], float(P), basef[:, :], ALU.mult, ALU.add)
                v.tensor_scalar(reg[:, E:E + 1], S[:, E - 1:E], -float(P), float(DUMMY), ALU.mult, ALU.add).then_inc(s_li, 1)
                dve.wait_ge(s_li, at + 11)
                v.tensor_tensor(dreg[:, :], reg[:, 1:E + 1], reg[:, 0:E], ALU.subtract).then_inc(s_li, 1)
                v.tensor_reduce(ek[:, 0:n], cmp[:, 0:n, :], X, ALU.add)
                dve.wait_ge(s_li, at + 12)
                v.tensor_tensor(pr[:, 0:n, :], cmp[:, 0:n, :], bc(dreg[:, None, :], [1, n, E]), ALU.mult).then_inc(s_li, 1)
                dve.wait_ge(s_li, at + 13)
                v.tensor_reduce(rr[:, 0:n], pr[:, 0:n, :], X, ALU.add).then_inc(s_li, 1)
                tail = dve.value_load(taili[0:1, 0:1], min_val=0, max_val=TILES)
                v.tensor_scalar(listE[:, bass.ds(tail, n)], ek[:, 0:n], float(E - 1), None, ALU.min)
                dve.wait_ge(s_li, at + 14)
                v.scalar_tensor_tensor(listR[:, bass.ds(tail, n)], rr[:, 0:n], reg[:, 0:1], cidx128[:, 0:n],
                                       ALU.add, ALU.add).then_inc(s_list, 1)
                v.tensor_copy(done[:, :], full[:, :]).then_inc(s_li, 1)
                v.tensor_tensor(tailf[:, :], tailf[:, :], S[:, E - 1:E], ALU.add).then_inc(s_li, 1)
                dve.wait_ge(s_li, at + 16)
                v.tensor_copy(taili[:, :], tailf[:, :]).then_inc(s_li, 1)
                dve.wait_ge(s_li, at + 17)

            def body(step, s, b, c):
                u = s * 2 + b
                xu = xall[:, bass.ds(u * (GB * D), GB * D)] if step in ("ADJ", "LN2") else None
                if step == "ADJ":
                    dve.wait_ge(s_adj[b], s * 16 + 16)
                    wait(dve, s_th, u * 2)
                    v.tensor_copy(adjb[:, :], adji[b][:, :]).then_inc(s_adjb, 1)
                if step == "MASK":
                    wait(dve, s_adjT, u + 1)
                    for k in range(KINDS):
                        last = v.tensor_single_scalar(mask[:, k, :], adjT[:, :], float(k + 1), ALU.is_equal)
                    last.then_inc(s_mask, 1)
                if step in ("E01", "E23"):
                    wait(dve, s_mask, u + 1)
                    wait(dve, s_clr, u + 1)
                    pair = 0 if step == "E01" else 1
                    at = (u * 2 + pair) * KINDS
                    wait(dve, s_e, u * GB + 2 * pair + 2)
                    into = sel[:, pair * 2 * P:(pair + 1) * 2 * P].rearrange("p (g i) -> p g i", g=2)
                    for k in range(KINDS):
                        if k:
                            dve.wait_ge(s_sel, at + k)
                        apart(dve)
                        v.copy_predicated(into, mask[:, k, pair * 2 * P:(pair + 1) * 2 * P].rearrange("p (g i) -> p g i", g=2),
                                          bE[:, :, k * P:(k + 1) * P]).then_inc(s_sel, 1)
                    if step == "E23":
                        dve.wait_ge(s_sel, at + KINDS)
                        wait(dve, s_tanh, u)
                        v.scalar_tensor_tensor(lk[:, :], sel[:, :], 0.2, sel[:, :], ALU.mult, ALU.max).then_inc(s_lk, 1)
                if step == "TANH":
                    wait(dve, s_tanh, u + 1)
                    v.tensor_single_scalar(al[:, :], al[:, :], 1.0, ALU.add).then_inc(s_al, 1)
                if step == "LN2":
                    wait(dve, s_go, u + 1)
                    wait(dve, s_xb, u + 1)
                    v.scalar_tensor_tensor(xu, bT[:, :], 0.5, xu, ALU.mult, ALU.add).then_inc(s_x1, 1)
                    more = not (isinstance(s, int) and u + 1 >= GROUPS)
                    if more:
                        dve.wait_ge(s_x[1 - b], (s + b) * 16 + 16)
                    dve.wait_ge(s_x1, u + 1)
                    norm((u + 1) * NORM, 0, 2 * GB if more else GB, lambda g: rows(u, g))
                    wait(dve, s_disp[b], s * (2 * GB * 16))
                    for g in range(GB):
                        last = apply(hxv[b][:, 0, g, 0:D], rows(u, g), g, g)
                    last.then_inc(s_h2, 1)
                    v.tensor_copy(hxv[b][:, :, :, D:D + 1].rearrange("p c g r -> p (c g) r").bitcast(U32),
                                  tok[:, bass.ds(u * (2 * GB), 2 * GB)])
                    if more:
                        first_norm(u + 1)
                    dve.wait_ge(s_h2, u + 1)
                    v.tensor_copy(hxv[b][:, 1, :, 0:D], hxv[b][:, 0, :, 0:D])
                if step == "ROUTE":
                    at = u * 14
                    wait(dve, s_lg, u + 1)
                    wait(dve, s_rt, at)
                    v.tensor_tensor(lg[:, :, :], bR[:, 0:GB * E].rearrange("p (g e) -> p g e", g=GB),
                                    bc(gbr[:, None, :], [P, GB, E]), ALU.add).then_inc(s_rt, 1)
                    dve.wait_ge(s_rt, at + 1)
                    one_hot_of_max(lg, m1, oh1, at + 1)
                    v.scalar_tensor_tensor(lg2[:, :, :], oh1[:, :, :], NEG, lg[:, :, :], ALU.mult, ALU.add).then_inc(s_rt, 1)
                    dve.wait_ge(s_rt, at + 7)
                    one_hot_of_max(lg2, m2, oh2, at + 7)
                    wait(dve, s_pf, u)
                    v.tensor_tensor(dsp[:, :].rearrange("p (g e) -> p g e", g=GB), oh1[:, :, :], oh2[:, :, :], ALU.add).then_inc(s_rt, 1)
                    v.tensor_tensor(dlt[:, :], m1[:, :], m2[:, :], ALU.subtract).then_inc(s_rt, 1)
                if step == "SLOT":
                    at = u * 6
                    wait(dve, s_pf, u + 1)
                    v.tensor_tensor(pos[:, :, :], bR[:, GB * E:2 * GB * E].rearrange("p (g e) -> p g e", g=GB),
                                    bc(run[:, None, :], [P, GB, E]), ALU.add).then_inc(s_so, 1)
                    dve.wait_ge(s_so, at + 1)
                    v.tensor_tensor(pm[:, 0, :, :], pos[:, :, :], oh1[:, :, :], ALU.mult).then_inc(s_so, 1)
                    v.tensor_tensor(pm[:, 1, :, :], pos[:, :, :], oh2[:, :, :], ALU.mult).then_inc(s_so, 1)
                    v.tensor_tensor(run[:, :], run[:, :], bR[:, 2 * GB * E:2 * GB * E + E], ALU.add).then_inc(s_so, 1)
                    dve.wait_ge(s_so, at + 3)
                    v.tensor_reduce(slotf[:, :, :], pm[:, :, :, :], X, ALU.add).then_inc(s_so, 1)
                    dve.wait_ge(s_so, at + 5)
                    wait(dve, s_disp[b], s * (2 * GB * 16))
                    v.tensor_copy(slot[b][:, :], slotf[:, :, :].rearrange("p c g -> p (c g)")).then_inc(s_so, 1)
                    wait(dve, s_gt, u + 1)
                    v.tensor_scalar(hxv[b][:, 0, :, D + 1], th[:, :], 0.5, 0.5, ALU.mult, ALU.add)
                    v.tensor_scalar(hxv[b][:, 1, :, D + 1], th[:, :], -0.5, 0.5, ALU.mult, ALU.add).then_inc(s_gate, 1)
                if step == "LIST":
                    dve.wait_ge(s_so, u * 6 + 6)
                    final = isinstance(s, int) and u == GROUPS - 1
                    append(u, final)
                    if final:
                        dve.wait_ge(s_dummy, 16)
                        v.tensor_copy(padx[:, :, D:D + 1].bitcast(U32), padi2[:, :]).then_inc(s_padi, 1)
                        v.tensor_scalar(pslot[:, :], run[:, :], iop[:, 0:1], None, ALU.add).then_inc(s_padi, 1)
                if step == "F":
                    h_ = c - 1
                    if has(s, h_):
                        wait(dve, s_sl, tile(s, h_) + 1)
                        wait(dve, s_tp, tile(s, h_) + 2)
                        v.tensor_tensor(hid[h_ % 2][:, :], sl[h_ % 2][:, :], bH[h_ % 2][:, HID:2 * HID], ALU.mult).then_inc(s_hid, 1)

            dve.wait_ge(s_x[0], 16)
            norm(0, GB, 2 * GB, lambda g: rows(0, g - GB))
            first_norm(0)
            program(dve, body)

            yin = [w12[:, r * 1024:(r + 1) * 1024].rearrange("p (g c d) -> p g c d", g=GB, c=2) for r in range(4)]
            yout = [w3s[:, r * 512:(r + 1) * 512].rearrange("p (g d) -> p g d", g=GB) for r in range(4)]

            def combine(t, r):
                dve.wait_ge(s_yin[r], t * 16 + 16)
                wait(dve, s_out[r], t * 16)
                xv = xall[:, bass.ds(t * (4 * GB * D) + r * GB * D, GB * D)].rearrange("p (g d) -> p g d", g=GB)
                v.tensor_tensor(yout[r], yin[r][:, :, 0, :], yin[r][:, :, 1, :], ALU.add).then_inc(s_a1, 1)
                dve.wait_ge(s_a1, t * 4 + (r + 1))
                v.tensor_tensor(yout[r], yout[r], xv, ALU.add).then_inc(s_a2, 1)

            dve.wait_ge(s_o, TILES)
            for r in range(4):
                combine(0, r)
            with dve.Fori(1, GROUPS // 4) as t:
                for r in range(4):
                    combine(t, r)


_INS = ["x", "adj", "L0_gnn_a0", "L0_gnn_a1", "L0_gnn_a2", "L0_gnn_a3", "L0_gnn_bias", "L0_ffn_gate_w", "L0_ffn_gate_b",
        "L0_ffn_w1", "L0_ffn_w2", "L0_ffn_w3"]


def kernel(**inputs):
    import numpy as _np
    import concourse.bacc as _bacc
    from concourse import mybir as _mybir
    from concourse.bass_utils import run_bass_kernel_spmd as _run

    nc = _bacc.Bacc("TRN2", target_bir_lowering=False, num_devices=1)
    arrays, args = {}, []
    for name in _INS:
        a = _np.ascontiguousarray(inputs[name])
        arrays[f"in_{name}"] = a
        args.append(nc.dram_tensor(f"in_{name}", a.shape, _mybir.dt.from_np(a.dtype), kind="ExternalInput").ap())
    out = nc.dram_tensor("out_x", (G, P, D), _mybir.dt.float32, kind="ExternalOutput").ap()
    build(nc, *args, out)
    r = _run(nc, [arrays], core_ids=[0])
    return r.results[0]["out_x"]
```

```python
from contextlib import ExitStack

import concourse.bass as bass
from concourse import mybir

G, P, D = 128, 128, 128
E, HID = 16, 256
KINDS = 4
GB = 4
GROUPS = G // GB
EPS = 1e-5
NEG = -1.0e30
TOKENS = G * P
CAP = TOKENS + P
FULL_TILES = 2 * TOKENS // P
TILES = FULL_TILES + E - 1
DUMMY = E * CAP
XS_ROWS = DUMMY + E * P
Y_ROWS = 2 * TOKENS + 2 * E * P
ROW = D + 2
TPG = FULL_TILES // GROUPS
LAG = 7
RING = 16
YRING = 8
NEW = TPG + E - 1
LAST = TILES - (TPG * (GROUPS - 1) - (E - 1))
LIST = TILES + LAST
DEPTH = 4

ALU = mybir.AluOpType
ACT = mybir.ActivationFunctionType
F32 = mybir.dt.float32
BF16 = mybir.dt.bfloat16
U16 = mybir.dt.uint16
U32 = mybir.dt.uint32
I32 = mybir.dt.int32
X = mybir.AxisListType.X


def build(nc, x, adj, a0, a1, a2, a3, bias, gate_w, gate_b, w1, w2, w3, out):
    xs = nc.dram_tensor("dispatched", [XS_ROWS, ROW], F32, kind="Internal").ap()
    y = nc.dram_tensor("expert_rows", [Y_ROWS, D], F32, kind="Internal").ap()

    with ExitStack() as ctx:
        def sb(name, shape, dt=F32):
            return ctx.enter_context(nc.sbuf_tensor(name, shape, dt))

        def ps(name):
            return ctx.enter_context(nc.psum_tensor(name, [P, 512], F32))

        def sem(name):
            return ctx.enter_context(nc.semaphore(name))

        xall = sb("xall", [P, G * D])
        w12 = sb("w12", [P, E * 2 * HID])
        w3s = sb("w3s", [P, E * 2 * D])
        adji = [sb(f"adji{b}", [P, GB * P], I32) for b in range(2)]
        adjb = sb("adjb", [P, GB * P], BF16)
        st = sb("st", [P, 2 * GB, 6])
        mv = sb("mv", [P, 2 * GB, 2])
        ve = sb("ve", [P, 2 * GB])
        rs = sb("rs", [P, 2 * GB])
        nt = sb("nt", [P, 2 * GB])
        nmr = sb("nmr", [P, 2 * GB])
        hN = [sb(f"hN{b}", [P, GB * D]) for b in range(2)]
        hT = sb("hT", [P, GB * P])
        sc = sb("sc", [P, GB, KINDS, P])
        adjT = sb("adjT", [P, GB * P], BF16)
        mask = sb("mask", [P, KINDS, GB * P], U16)
        sel = sb("sel", [P, GB * P])
        lk = sb("lk", [P, GB * P])
        al = sb("al", [P, GB * P])
        hx = [sb(f"hx{b}", [P, 2 * GB * ROW]) for b in range(2)]
        h2T = sb("h2T", [P, GB * P])
        lg = sb("lg", [P, GB, E])
        lg2 = sb("lg2", [P, GB, E])
        eq = sb("eq", [P, GB, E])
        wq = sb("wq", [P, GB, E])
        oh1 = sb("oh1", [P, GB, E])
        oh2 = sb("oh2", [P, GB, E])
        m1 = sb("m1", [P, GB])
        m2 = sb("m2", [P, GB])
        mx = sb("mx", [P, GB])
        dlt = sb("dlt", [P, GB])
        th = sb("th", [P, GB])
        dsp = sb("dsp", [P, GB * E], BF16)
        pos = sb("pos", [P, GB, E])
        pm = sb("pm", [P, 2, GB, E])
        slotf = sb("slotf", [P, 2, GB])
        slot = [sb(f"slot{b}", [P, 2 * GB], U32) for b in range(2)]
        run = sb("run", [P, E])
        tok = sb("tok", [P, GROUPS * 2 * GB], I32)
        xg = [sb(f"xg{r}", [P, ROW]) for r in range(RING)]
        xh = [sb(f"xh{b}", [P, 3 * P]) for b in range(2)]
        sl = [sb(f"sl{b}", [P, HID]) for b in range(2)]
        hid = [sb(f"hid{b}", [P, HID]) for b in range(2)]
        yo = [sb(f"yo{r}", [P, D]) for r in range(YRING)]
        padx = sb("padx", [P, E, ROW])
        padi = sb("padi", [P, E], I32)
        padi2 = sb("padi2", [P, E], I32)
        pslot = sb("pslot", [P, E], U32)
        basef = sb("basef", [1, E])
        cnti = sb("cnti", [1, E], I32)
        cnth = sb("cnth", [1, E], I32)
        full = sb("full", [1, E])
        done = sb("done", [1, E])
        new = sb("new", [1, E])
        pre = [sb(f"pre{i}", [1, 2 * E]) for i in range(2)]
        sx = sb("sx", [1, E])
        reg = sb("reg", [1, E + 1])
        dreg = sb("dreg", [1, E])
        cmp = sb("cmp", [1, LAST, E])
        pr = sb("pr", [1, LAST, E])
        ek = sb("ek", [1, LAST])
        rr = sb("rr", [1, LAST])
        cidx = sb("cidx", [1, LAST])
        cidx128 = sb("cidx128", [1, LAST])
        listE = sb("listE", [1, LIST], I32)
        listR = sb("listR", [1, LIST], I32)
        tailf = sb("tailf", [1, 1])
        taili = sb("taili", [1, 1], I32)
        ident = sb("ident", [P, P])
        identb = sb("identb", [P, P], BF16)
        tri = sb("tri", [P, P], BF16)
        ones = sb("ones", [P, P], BF16)
        acol = sb("acol", [P, KINDS])
        biasr = sb("biasr", [P, D])
        bres = sb("bres", [P, D])
        bpart = sb("bpart", [P, D], BF16)
        bias3 = sb("bias3", [P, GB * D], BF16)
        gw = sb("gw", [P, E])
        gbr = sb("gbr", [P, E])
        wt = sb("wt", [P, E])
        iop = sb("iop", [P, 1])

        bE = ctx.enter_context(nc.psum_tensor("bE", [P, 2, 512], F32))
        bT, bR, bH0, bH1, bXH, bO = [ps(n) for n in ("bT", "bR", "bH0", "bH1", "bXH", "bO")]
        bH = [bH0, bH1]
        adjTp = bR[:, GB * P // 2:GB * P].bitcast(BF16)

        s_x = [sem(f"x_landed{b}") for b in range(2)]
        s_adj = [sem(f"adj_landed{b}") for b in range(2)]
        s_w = sem("weights_landed")
        s_small = sem("small_landed")
        s_c = sem("pool_constants")
        s_cv = sem("dve_constants")
        s_pad0 = sem("pads_built")
        s_dummy = sem("dummy_tiles_stored")
        s_ln = sem("norm_steps")
        s_stat = [sem(f"row_statistics{h}") for h in range(2)]
        s_h = sem("h_written")
        s_adjb = sem("adj_cast")
        s_th = sem("h_transposed")
        s_sc = sem("h_scaled")
        s_adjT = sem("adjT_copied")
        s_mask = sem("masks")
        s_clr = sem("sel_cleared")
        s_e = sem("e_ready")
        s_sel = sem("e_selected")
        s_lk = sem("leaky")
        s_tanh = sem("tanh")
        s_al = sem("alpha")
        s_go = sem("gnn_out")
        s_bias = sem("bias_split_steps")
        s_hx = sem("second_rows_copied")
        s_x1 = sem("x1_written")
        s_h2 = sem("h2_written")
        s_t2 = sem("h2_transposed")
        s_h2T = sem("h2T_copied")
        s_lg = sem("logits")
        s_rt = sem("route_steps")
        s_gt = sem("gate_tanh")
        s_gate = sem("gates_written")
        s_pf = sem("prefix")
        s_so = sem("slot_steps")
        s_li = sem("list_steps")
        s_list = sem("list_appended")
        s_disp = [sem(f"dispatched{b}") for b in range(2)]
        s_padi = sem("pad_slots")
        s_pads = sem("pads_stored")
        s_xg = [sem(f"tile_landed{r}") for r in range(RING)]
        s_tp = sem("tile_transposed")
        s_xh = sem("tile_transposes_copied")
        s_hp = sem("h_products")
        s_sl = sem("silu")
        s_hid = sem("hidden")
        s_o = sem("expert_out")
        s_yo = sem("expert_out_gated")
        s_y = [sem(f"rows_stored{r}") for r in range(YRING)]
        s_apart = sem("waits_taken_apart")
        s_yin = [sem(f"y_loaded{r}") for r in range(4)]
        s_a1 = sem("first_sum")
        s_a2 = sem("second_sum")
        s_out = [sem(f"out_stored{r}") for r in range(4)]

        block = ctx.enter_context(nc.Block())

        def wait(eng, s, count):
            if not isinstance(count, int) or count > 0:
                eng.wait_ge(s, count)

        def apart(eng):
            eng.sem_inc(s_apart, 1)

        def bc(ap, shape):
            return ap.to_broadcast(shape)

        ALL = 1000
        ORDER = [("F", 0), ("T1", 0), ("EVA", 0), ("RA", 3), ("NB", 1), ("MIX", 7), ("D3", 4),
                 ("F", 1), ("EVB", 0), ("MIX", ALL),
                 ("F", 2), ("EVC", 0), ("GT", 3), ("MASK", 0), ("LIST", 4), ("MIX", 9),
                 ("F", 3), ("PREF", 3), ("E01", 0), ("H2", 2), ("MIX", ALL), ("PADS", 4),
                 ("F", 4), ("CP01", 0), ("MIX", ALL), ("SLOT", 3), ("HX", 2), ("T2", 2), ("H2T", 2), ("D0", 3),
                 ("F", 5), ("OUT", 1), ("E23", 0), ("NX", -2), ("D1", 3),
                 ("F", 6), ("X1", 1), ("CP23", 0), ("MIX", 4), ("H1", -1), ("LOG", 2), ("D2", 3),
                 ("F", 7), ("MIX", ALL), ("LG", 2), ("NY", 1), ("TANH", 0), ("ADJ", -1), ("LOAD", 0)]
        NORMS = ("NB",)
        LAST_S = (TILES - 1 + DEPTH + TPG * LAG) // (2 * TPG)

        def walk(fn, s, first, last):
            for b in range(2):
                for step, back in ORDER:
                    if step == "F":
                        c = TPG * (b - LAG) + back
                        if 2 * TPG * last + c >= 0 and 2 * TPG * first + c < TILES + DEPTH:
                            fn("F", s, b, c)
                        continue
                    if step == "MIX":
                        fn("MIX", s, b, back)
                        continue
                    at = b - back
                    lo, hi = 2 * first + at, 2 * last + at
                    if hi >= 0 and lo < (GROUPS + 1 if step in NORMS else GROUPS):
                        fn(step, s + at // 2 if at // 2 else s, at % 2, None)

        LOOP = (5, GROUPS // 2 - 2)

        def program(eng, fn):
            for s in range(LOOP[0]):
                walk(fn, s, s, s)
            with eng.Fori(LOOP[0], LOOP[1]) as s:
                walk(fn, s, LOOP[0], LOOP[1] - 1)
            for s in range(LOOP[1], LAST_S + 1):
                walk(fn, s, s, s)

        def has(s, c):
            return not isinstance(s, int) or 0 <= 2 * TPG * s + c < TILES

        def tile(s, c):
            return s * (2 * TPG) + c

        def lap(s, c, ring):
            per = 2 * TPG // ring
            return s * per + (c // ring) + 1

        NORM = 13
        LI = 17
        hxv = [h[:, :].rearrange("p (c g r) -> p c g r", c=2, r=ROW) for h in hx]

        @block.sync
        def _(sp):
            x_g = x.rearrange("g p d -> p g d")
            adj_g = adj.rearrange("g i j -> i g j")

            def load_x(u, b):
                sp.dma_start(xall[:, bass.ds(u * (GB * D), GB * D)].rearrange("p (g d) -> p g d", g=GB),
                             x_g[:, bass.ds(u * GB, GB), :]).then_inc(s_x[b], 16)

            def load_adj(u, b):
                sp.dma_start(adji[b][:, :].rearrange("p (g d) -> p g d", g=GB),
                             adj_g[:, bass.ds(u * GB, GB), :]).then_inc(s_adj[b], 16)

            load_x(0, 0)
            load_adj(0, 0)
            sp.dma_start(acol[:, 0:1], a0).then_inc(s_small, 16)
            sp.dma_start(acol[:, 1:2], a1).then_inc(s_small, 16)
            sp.dma_start(acol[:, 2:3], a2).then_inc(s_small, 16)
            sp.dma_start(acol[:, 3:4], a3).then_inc(s_small, 16)
            sp.dma_start(biasr[:, :], bias.rearrange("(a d) -> a d", a=1).to_broadcast([P, D])).then_inc(s_small, 16)
            sp.dma_start(gbr[:, :], gate_b.rearrange("(a d) -> a d", a=1).to_broadcast([P, E])).then_inc(s_small, 16)
            sp.dma_start(gw[:, :], gate_w).then_inc(s_small, 16)
            load_x(1, 1)
            load_adj(1, 1)
            w12v = w12[:, :].rearrange("p (e w h) -> p e w h", e=E, w=2)
            sp.wait_ge(s_x[0], 16)
            load_x(2, 0)
            sp.dma_start(w12v[:, :, 0, :], w1.rearrange("e d h -> d e h")).then_inc(s_w, 16)
            sp.dma_start(w12v[:, :, 1, :], w2.rearrange("e d h -> d e h")).then_inc(s_w, 16)
            sp.dma_start(w3s[:, :].rearrange("p (e c o) -> p e c o", e=E, c=2),
                         w3.rearrange("e (c p) o -> p e c o", c=2)).then_inc(s_w, 16)
            sp.wait_ge(s_pad0, 1)
            sp.dma_start(xs[DUMMY:DUMMY + E * P, :].rearrange("(e p) r -> p e r", p=P), padx[:, :, :]).then_inc(s_dummy, 16)
            sp.wait_ge(s_dummy, 16)

            def body(step, s, b, c):
                u = s * 2 + b
                if step == "LOAD":
                    if not (isinstance(s, int) and u + 2 >= GROUPS):
                        wait(sp, s_adjb, u + 1)
                        apart(sp)
                        load_adj(u + 2, b)
                    if not (isinstance(s, int) and u + 3 >= GROUPS):
                        wait(sp, s_x[1 - b], (s + b) * 16 + 16)
                        apart(sp)
                        load_x(u + 3, 1 - b)
                if step == "F" and has(s, c):
                    if (c + TPG * LAG) % TPG == 0:
                        if not (isinstance(s, int) and u - 4 > GROUPS):
                            wait(sp, s_list, u - 4)
                            apart(sp)
                            wait(sp, s_disp[1 - b], (s - 2 + b) * (2 * GB * 16))
                        if isinstance(s, int) and u == GROUPS + 4:
                            sp.wait_ge(s_pads, 16 * E)
                    row = sp.value_load(listR[0:1, bass.ds(tile(s, c), 1)], min_val=0, max_val=XS_ROWS - P)
                    wait(sp, s_y[c % YRING], 16 * lap(s, c - RING, YRING))
                    sp.dma_start(xg[c % RING][:, :], xs[bass.ds(row, P), :]).then_inc(s_xg[c % RING], 16)

            program(sp, body)

            yin = [w12[:, r * 1024:(r + 1) * 1024] for r in range(4)]
            y_g = y[0:2 * TOKENS, :].rearrange("(g p c) d -> p g (c d)", p=P, c=2)
            for r in range(YRING):
                last = max(t for t in range(TILES) if t % YRING == r)
                sp.wait_ge(s_y[r], 16 * (last // YRING + 1))
            sp.wait_ge(s_hp, TILES)
            for r in range(4):
                sp.dma_start(yin[r].rearrange("p (g d) -> p g d", g=GB), y_g[:, r * GB:(r + 1) * GB, :]).then_inc(s_yin[r], 16)
            with sp.Fori(1, GROUPS // 4) as t:
                for r in range(4):
                    sp.wait_ge(s_a2, t * 4 + (r - 3))
                    sp.dma_start(yin[r].rearrange("p (g d) -> p g d", g=GB),
                                 y_g[:, bass.ds(t * (4 * GB) + r * GB, GB), :]).then_inc(s_yin[r], 16)

        @block.gpsimd
        def _(pool):
            nc.gpsimd.memset(ident[:, :], 0.0).then_inc(s_c, 1)
            nc.gpsimd.memset(identb[:, :], 0.0).then_inc(s_c, 1)
            nc.gpsimd.memset(tri[:, :], 1.0).then_inc(s_c, 1)
            nc.gpsimd.memset(ones[:, :], 1.0).then_inc(s_c, 1)
            nc.gpsimd.memset(padx[:, :, :], 0.0).then_inc(s_c, 1)
            nc.gpsimd.memset(bias3[:, :], 0.0).then_inc(s_c, 1)
            nc.gpsimd.iota(wt[:, :], pattern=[[-1, E]], base=E, channel_multiplier=0,
                           allow_small_or_imprecise_dtypes=True).then_inc(s_c, 1)
            nc.gpsimd.iota(iop[:, :], pattern=[[0, 1]], base=0, channel_multiplier=1,
                           allow_small_or_imprecise_dtypes=True).then_inc(s_c, 1)
            nc.gpsimd.iota(run[:, :], pattern=[[CAP, E]], base=0, channel_multiplier=0,
                           allow_small_or_imprecise_dtypes=True).then_inc(s_c, 1)
            nc.gpsimd.iota(basef[:, :], pattern=[[CAP, E]], base=0, channel_multiplier=0,
                           allow_small_or_imprecise_dtypes=True).then_inc(s_c, 1)
            nc.gpsimd.iota(cidx[:, :], pattern=[[1, LAST]], base=0, channel_multiplier=0,
                           allow_small_or_imprecise_dtypes=True).then_inc(s_c, 1)
            nc.gpsimd.iota(cidx128[:, :], pattern=[[P, LAST]], base=0, channel_multiplier=0,
                           allow_small_or_imprecise_dtypes=True).then_inc(s_c, 1)
            nc.gpsimd.iota(tok[:, :].rearrange("p (u c g) -> p u c g", c=2, g=GB),
                           pattern=[[2 * P * GB, GROUPS], [1, 2], [2 * P, GB]], base=0, channel_multiplier=2).then_inc(s_c, 1)
            nc.gpsimd.iota(padi[:, :], pattern=[[P, E]], base=2 * TOKENS, channel_multiplier=1).then_inc(s_c, 1)
            nc.gpsimd.iota(padi2[:, :], pattern=[[P, E]], base=2 * TOKENS + E * P, channel_multiplier=1).then_inc(s_c, 1)
            pool.wait_ge(s_c, 15)
            nc.gpsimd.affine_select(out=ident[:, :], in_=ident[:, :], compare_op=ALU.not_equal, fill=1.0,
                                    base=0, pattern=[[-1, P]], channel_multiplier=1).then_inc(s_c, 1)
            nc.gpsimd.affine_select(out=identb[:, :], in_=identb[:, :], compare_op=ALU.not_equal, fill=1.0,
                                    base=0, pattern=[[-1, P]], channel_multiplier=1).then_inc(s_c, 1)
            nc.gpsimd.affine_select(out=tri[:, :], in_=tri[:, :], compare_op=ALU.is_gt, fill=0.0,
                                    base=0, pattern=[[1, P]], channel_multiplier=-1).then_inc(s_c, 1)

            def body(step, s, b, c):
                u = s * 2 + b
                if step == "T1":
                    wait(pool, s_lk, u)
                    apart(pool)
                    nc.gpsimd.memset(sel[:, :], NEG).then_inc(s_clr, 1)
                if step in ("D0", "D1", "D2", "D3"):
                    if step == "D0":
                        pool.wait_ge(s_hx, u + 1)
                        pool.wait_ge(s_gate, u + 1)
                        apart(pool)
                    for n in range(2 * int(step[1]), 2 * int(step[1]) + 2):
                        nc.gpsimd.indirect_dma_start(
                            out=xs[:, :], out_offset=bass.IndirectOffsetOnAxis(ap=slot[b][:, n:n + 1], axis=0),
                            in_=hx[b][:, n * ROW:(n + 1) * ROW], in_offset=None).then_inc(s_disp[b], 16)
                if step == "PADS" and isinstance(s, int) and u == GROUPS - 1:
                    pool.wait_ge(s_padi, 2)
                    for e in range(E):
                        nc.gpsimd.indirect_dma_start(
                            out=xs[:, :], out_offset=bass.IndirectOffsetOnAxis(ap=pslot[:, e:e + 1], axis=0),
                            in_=padx[:, e, :], in_offset=None).then_inc(s_pads, 16)
                if step == "F" and has(s, c - DEPTH):
                    o = c - DEPTH
                    wait(pool, s_yo, tile(s, o) + 1)
                    apart(pool)
                    nc.gpsimd.indirect_dma_start(
                        out=y[:, :],
                        out_offset=bass.IndirectOffsetOnAxis(ap=xg[o % RING][:, D:D + 1].bitcast(U32), axis=0),
                        in_=yo[o % YRING][:, :], in_offset=None).then_inc(s_y[o % YRING], 16)

            program(pool, body)

        @block.tensor
        def _(pe):
            pe.wait_ge(s_c, 18)
            pe.wait_ge(s_small, 16 * 7)

            def body(step, s, b, c):
                u = s * 2 + b
                if step == "T1":
                    wait(pe, s_h, u + 1)
                    wait(pe, s_x1, u - 1)
                    for g in range(GB):
                        last = nc.tensor.transpose(bT[:, g * P:(g + 1) * P], hN[b][:, g * D:(g + 1) * D], ident[:, :])
                    last.then_inc(s_th, 1)
                    wait(pe, s_adjb, u + 1)
                    wait(pe, s_adjT, u)
                    wait(pe, s_rt, u * 14 - 41)
                    for g in range(GB):
                        last = nc.tensor.transpose(adjTp[:, g * P:(g + 1) * P], adjb[:, g * P:(g + 1) * P], identb[:, :])
                    last.then_inc(s_th, 1)
                if step in ("E01", "E23"):
                    wait(pe, s_sc, u + 1)
                    pair = 0 if step == "E01" else 1
                    wait(pe, s_sel, (u * 2 + pair) * KINDS)
                    for g in (2 * pair, 2 * pair + 1):
                        nc.tensor.matmul(bE[:, g % 2, :], hT[:, g * P:(g + 1) * P], sc[:, g, :, :].rearrange("p k i -> p (k i)"),
                                         start=True, stop=True).then_inc(s_e, 1)
                if step == "OUT":
                    if isinstance(s, int) and u == 0:
                        pe.wait_ge(s_bias, 8)
                    wait(pe, s_h2T, u)
                    nc.tensor.matmul(bT[:, :], ones[:, :], bias3[:, :], start=True, stop=False, skip_group_check=True)
                    wait(pe, s_al, u + 1)
                    for g in range(GB):
                        last = nc.tensor.matmul(bT[:, g * D:(g + 1) * D], al[:, g * P:(g + 1) * P], hN[b][:, g * D:(g + 1) * D],
                                                start=False, stop=True, skip_group_check=True)
                    last.then_inc(s_go, 1)
                if step == "T2":
                    wait(pe, s_h2, u + 1)
                    wait(pe, s_sc, (u + 3) if not (isinstance(s, int) and u + 2 >= GROUPS) else GROUPS)
                    for g in range(GB):
                        last = nc.tensor.transpose(bT[:, g * P:(g + 1) * P], hxv[b][:, 0, g, 0:D], ident[:, :])
                    last.then_inc(s_t2, 1)
                if step == "LOG":
                    wait(pe, s_h2T, u + 1)
                    wait(pe, s_so, u * 6)
                    for g in range(GB):
                        last = nc.tensor.matmul(bR[:, g * E:(g + 1) * E], h2T[:, g * P:(g + 1) * P], gw[:, :], start=True, stop=True)
                    last.then_inc(s_lg, 1)
                if step == "PREF":
                    wait(pe, s_rt, u * 14 + 13)
                    wait(pe, s_adjT, (u + 4) if not (isinstance(s, int) and u + 3 >= GROUPS) else GROUPS)
                    n = GB * E
                    nc.tensor.matmul(bR[:, n:2 * n], tri[:, :], dsp[:, :], start=True, stop=False, skip_group_check=True)
                    for g in range(1, GB):
                        nc.tensor.matmul(bR[:, n + g * E:2 * n], ones[:, :], dsp[:, 0:n - g * E], start=False, stop=(g == GB - 1),
                                         skip_group_check=True)
                    for g in range(GB):
                        last = nc.tensor.matmul(bR[:, 2 * n:2 * n + E], ones[:, :], dsp[:, g * E:(g + 1) * E],
                                                start=False, stop=(g == GB - 1), skip_group_check=True)
                    last.then_inc(s_pf, 1)
                if step == "F":
                    slot_f(s, b, c)

            held = {}

            def expert(s, c):
                if c not in held:
                    held[c] = nc.values_load(listE[0:1, bass.ds(tile(s, c), 1)], engines=[mybir.EngineType.PE],
                                             min_val=0, max_val=E - 1,
                                             skip_runtime_bounds_check_because="the list holds experts only")
                return held[c]

            def slot_f(s, b, c):
                u = s * 2 + b
                x_, h_, t_, o_ = c, c - 1, c - 3, c - DEPTH
                if (c + TPG * LAG) % (2 * TPG) == 0:
                    held.clear()
                if isinstance(s, int) and tile(s, c) == 0:
                    pe.wait_ge(s_w, 48)
                if has(s, x_) or has(s, t_):
                    if (c + TPG * LAG) % TPG == 0 and not (isinstance(s, int) and u - 4 > GROUPS):
                        wait(pe, s_list, u - 4)
                    wait(pe, s_xh, tile(s, c))
                    last = None
                    if has(s, x_):
                        wait(pe, s_xg[x_ % RING], 16 * lap(s, x_, RING))
                        last = nc.tensor.transpose(bXH[:, 0:P], xg[x_ % RING][:, 0:D], ident[:, :])
                    if has(s, t_):
                        wait(pe, s_hid, tile(s, t_) + 1)
                        for h in range(2):
                            last = nc.tensor.transpose(bXH[:, (1 + h) * P:(2 + h) * P], hid[t_ % 2][:, h * P:(h + 1) * P], ident[:, :])
                    last.then_inc(s_tp, 1)
                if has(s, h_):
                    e = expert(s, h_)
                    wait(pe, s_xh, tile(s, h_) + 1)
                    wait(pe, s_hid, tile(s, h_) - 1)
                    nc.tensor.matmul(bH[h_ % 2][:, :], xh[h_ % 2][:, 0:P], w12[:, bass.ds(e * (2 * HID), 2 * HID)],
                                     start=True, stop=True).then_inc(s_hp, 1)
                e = expert(s, o_) if has(s, o_) else None
                if has(s, x_) and (c + TPG * LAG) % (2 * TPG) != 2 * TPG - 1:
                    expert(s, x_)
                if has(s, o_):
                    wait(pe, s_xh, tile(s, c))
                    wait(pe, s_yo, tile(s, o_))
                    for h in range(2):
                        last = nc.tensor.matmul(bO[:, 0:D], xh[(c - 1) % 2][:, (1 + h) * P:(2 + h) * P],
                                                w3s[:, bass.ds(e * (2 * D) + h * D, D)], start=(h == 0), stop=(h == 1))
                    last.then_inc(s_o, 1)

            program(pe, body)

        @block.scalar
        def _(act):
            act.wait_ge(s_small, 16 * 7)

            def scaled(k):
                nc.scalar.activation(sc[:, :, k, :], bT[:, :].rearrange("p (g i) -> p g i", g=GB), ACT.Copy,
                                     scale=acol[:, k:k + 1])

            def apply(into, u, g, n):
                return nc.scalar.activation(into, xall[:, bass.ds(u * (GB * D) + g * D, D)], ACT.Identity,
                                            bias=nmr[:, n:n + 1], scale=rs[:, n:n + 1])

            def body(step, s, b, c):
                u = s * 2 + b
                if step == "EVA":
                    wait(act, s_th, u * 2 + 2)
                    wait(act, s_mask, u)
                    nc.scalar.activation(adjT[:, :], adjTp[:, :], ACT.Copy).then_inc(s_adjT, 1)
                    wait(act, s_e, u * GB)
                    scaled(0)
                if step == "EVB":
                    scaled(1)
                    scaled(2)
                if step == "EVC":
                    scaled(3)
                    nc.scalar.activation(hT[:, :], bT[:, :], ACT.Copy).then_inc(s_sc, 1)
                if step == "H2":
                    act.wait_ge(s_ln, (u + 3) * NORM + NORM)
                    wait(act, s_disp[b], s * (2 * GB * 16))
                    for g in range(GB):
                        last = apply(hxv[b][:, 0, g, 0:D], u, g, g)
                    last.then_inc(s_h2, 1)
                if step == "HX":
                    wait(act, s_h2, u + 1)
                    nc.scalar.activation(hxv[b][:, 1, :, 0:D], hxv[b][:, 0, :, 0:D], ACT.Copy).then_inc(s_hx, 1)
                if step == "H1":
                    wait(act, s_ln, u * NORM + NORM)
                    wait(act, s_go, u - 1)
                    for g in range(GB):
                        last = apply(hN[b][:, g * D:(g + 1) * D], u, g, GB + g)
                    last.then_inc(s_h, 1)
                if step == "GT":
                    wait(act, s_rt, u * 14 + 14)
                    wait(act, s_gate, u)
                    nc.scalar.activation(th[:, :], dlt[:, :], ACT.Tanh, scale=0.5).then_inc(s_gt, 1)
                if step == "TANH":
                    wait(act, s_lk, u + 1)
                    wait(act, s_go, u)
                    nc.scalar.activation(al[:, :], lk[:, :], ACT.Tanh, scale=0.5).then_inc(s_tanh, 1)
                    act.wait_ge(s_tanh, u + 1)
                    nc.scalar.activation(al[:, :], al[:, :], ACT.Copy, bias=1.0).then_inc(s_al, 1)
                if step == "ADJ":
                    act.wait_ge(s_adj[b], s * 16 + 16)
                    wait(act, s_th, u * 2)
                    nc.scalar.activation(adjb[:, :], adji[b][:, :], ACT.Copy).then_inc(s_adjb, 1)
                if step == "H2T":
                    wait(act, s_t2, u + 1)
                    wait(act, s_lg, u)
                    nc.scalar.activation(h2T[:, :], bT[:, :], ACT.Copy).then_inc(s_h2T, 1)
                if step == "F":
                    x_, h_, t_, o_ = c, c - 1, c - 3, c - DEPTH
                    if has(s, x_) or has(s, t_):
                        lo = 0 if has(s, x_) else P
                        hi = 3 * P if has(s, t_) else P
                        wait(act, s_tp, tile(s, c) + 1)
                        wait(act, s_hp, tile(s, c) - 1 if has(s, c - 2) else 0)
                        wait(act, s_o, tile(s, c) - 4)
                        nc.scalar.activation(xh[c % 2][:, lo:hi], bXH[:, lo:hi], ACT.Copy).then_inc(s_xh, 1)
                    if has(s, h_):
                        wait(act, s_hp, tile(s, h_) + 1)
                        wait(act, s_hid, tile(s, h_) - 1)
                        nc.scalar.activation(sl[h_ % 2][:, :], bH[h_ % 2][:, 0:HID], ACT.Silu).then_inc(s_sl, 1)
                    if has(s, o_):
                        wait(act, s_o, tile(s, o_) + 1)
                        wait(act, s_y[o_ % YRING], 16 * (lap(s, o_, YRING) - 1))
                        nc.scalar.activation(yo[o_ % YRING][:, :], bO[:, 0:D], ACT.Copy,
                                             scale=xg[o_ % RING][:, D + 1:D + 2]).then_inc(s_yo, 1)

            body("ADJ", 0, 0, None)
            body("H1", 0, 0, None)
            program(act, body)

            yout = [w3s[:, r * 512:(r + 1) * 512] for r in range(4)]
            out_g = out.rearrange("g p d -> p g d")
            with act.Fori(0, GROUPS // 4) as t:
                for r in range(4):
                    act.wait_ge(s_a2, t * 4 + (r + 1))
                    act.dma_start(out_g[:, bass.ds(t * (4 * GB) + r * GB, GB), :],
                                  yout[r].rearrange("p (g d) -> p g d", g=GB)).then_inc(s_out[r], 16)
            for r in range(4):
                act.wait_ge(s_out[r], 16 * (GROUPS // 4))

        @block.vector
        def _(dve):
            v = nc.vector
            dve.wait_ge(s_c, 18)
            dve.wait_ge(s_small, 16 * 7)
            v.memset(done[:, :], 0.0)
            v.memset(pre[0][:, :], 0.0)
            v.memset(pre[1][:, :], 0.0)
            v.memset(tailf[:, :], 0.0)
            v.memset(taili[:, :], 0).then_inc(s_cv, 1)
            v.tensor_copy(padx[:, :, D:D + 1].bitcast(U32), padi[:, :]).then_inc(s_pad0, 1)
            dve.wait_ge(s_cv, 1)

            v.tensor_single_scalar(bres[:, :], biasr[:, :], 2.0, ALU.mult).then_inc(s_bias, 1)
            for i in range(3):
                dve.wait_ge(s_bias, 3 * i + 1 if i else 1)
                v.tensor_copy(bpart[:, :], bres[:, :]).then_inc(s_bias, 1)
                dve.wait_ge(s_bias, 3 * i + 2)
                v.tensor_copy(bias3[32 * i:32 * i + 1, :].rearrange("p (g d) -> p g d", g=GB),
                              bc(bpart[32 * i:32 * i + 1, None, :], [1, GB, D])).then_inc(s_bias, 1)
                if i < 2:
                    v.tensor_tensor(bres[:, :], bres[:, :], bpart[:, :], ALU.subtract).then_inc(s_bias, 1)
                dve.wait_ge(s_bias, 3 * i + (4 if i < 2 else 3))

            def parts(s, b):
                u = s * 2 + b
                x1_too = not (isinstance(s, int) and u < 1)
                x_too = not (isinstance(s, int) and u + 2 >= GROUPS)
                return (0 if x1_too else GB), (2 * GB if x_too else GB)

            def statistics(s, b, half):
                u = s * 2 + b
                if half:
                    dve.wait_ge(s_x[b], s * 16 + 16)
                else:
                    dve.wait_ge(s_x1, u + 1)
                apart(dve)
                for g in range(GB):
                    last = v.bn_stats(st[:, half * GB + g, :], rows(u, g))
                last.then_inc(s_stat[half], 1)

            def norm_b(s, b):
                lo, hi = parts(s, b)
                t = s * 2 + b + 2
                at = t * NORM
                if hi > GB:
                    dve.wait_ge(s_stat[1], t + 1)
                if lo == 0:
                    dve.wait_ge(s_stat[0], t - 2)
                wait(dve, s_ln, at)
                apart(dve)
                for g in range(lo, hi):
                    last = v.bn_aggr(mv[:, g, :], st[:, g, :])
                last.then_inc(s_ln, 1)
                yield
                dve.wait_ge(s_ln, at + 1)
                v.tensor_single_scalar(ve[:, lo:hi], mv[:, lo:hi, 1], EPS, ALU.add).then_inc(s_ln, 1)
                yield
                V, R, T = ve[:, lo:hi], rs[:, lo:hi], nt[:, lo:hi]
                dve.wait_ge(s_ln, at + 2)
                wait(dve, s_h, min(t, GROUPS) if isinstance(t, int) else t)
                wait(dve, s_h2, t - 3)
                v.tensor_scalar(R.bitcast(I32), V.bitcast(I32), -0.5, 1597463007.0, ALU.mult, ALU.add).then_inc(s_ln, 1)
                yield
                for i in range(3):
                    dve.wait_ge(s_ln, at + 3 + 3 * i)
                    v.scalar_tensor_tensor(T, R, -0.5, R, ALU.mult, ALU.mult).then_inc(s_ln, 1)
                    yield
                    dve.wait_ge(s_ln, at + 4 + 3 * i)
                    v.tensor_tensor(T, T, V, ALU.mult).then_inc(s_ln, 1)
                    yield
                    dve.wait_ge(s_ln, at + 5 + 3 * i)
                    v.scalar_tensor_tensor(R, T, 1.5, R, ALU.add, ALU.mult).then_inc(s_ln, 1)
                    yield
                dve.wait_ge(s_ln, at + 12)
                v.scalar_tensor_tensor(nmr[:, lo:hi], mv[:, lo:hi, 0], -1.0, R, ALU.mult, ALU.mult).then_inc(s_ln, 1)
                yield

            def rows(u, g):
                return xall[:, bass.ds(u * (GB * D) + g * D, D)]

            def one_hot_of_max(src, m, oh, base):
                dve.wait_ge(s_rt, base)
                v.tensor_reduce(m[:, :], src[:, :, :], X, ALU.max).then_inc(s_rt, 1)
                yield
                dve.wait_ge(s_rt, base + 1)
                v.tensor_tensor(eq[:, :, :], src[:, :, :], bc(m[:, :, None], [P, GB, E]), ALU.is_equal).then_inc(s_rt, 1)
                yield
                dve.wait_ge(s_rt, base + 2)
                v.tensor_tensor(wq[:, :, :], eq[:, :, :], bc(wt[:, None, :], [P, GB, E]), ALU.mult).then_inc(s_rt, 1)
                yield
                dve.wait_ge(s_rt, base + 3)
                v.tensor_reduce(mx[:, :], wq[:, :, :], X, ALU.max).then_inc(s_rt, 1)
                yield
                dve.wait_ge(s_rt, base + 4)
                v.tensor_tensor(oh[:, :, :], wq[:, :, :], bc(mx[:, :, None], [P, GB, E]), ALU.is_equal).then_inc(s_rt, 1)
                yield

            def append(u, final):
                n = LAST if final else NEW
                at = u * LI
                wait(dve, s_so, u * 6 + 6)
                wait(dve, s_li, at)
                v.tensor_tensor(cnti[:, :], run[0:1, :], basef[:, :], ALU.subtract).then_inc(s_li, 1)
                yield
                dve.wait_ge(s_li, at + 1)
                if final:
                    v.tensor_single_scalar(cnti[:, :], cnti[:, :], P - 1, ALU.add).then_inc(s_cv, 1)
                    dve.wait_ge(s_cv, 2)
                v.tensor_single_scalar(cnth[:, :], cnti[:, :], 7, ALU.arith_shift_right).then_inc(s_li, 1)
                yield
                dve.wait_ge(s_li, at + 2)
                v.tensor_copy(full[:, :], cnth[:, :]).then_inc(s_li, 1)
                yield
                dve.wait_ge(s_li, at + 3)
                v.tensor_tensor(pre[0][:, E:2 * E], full[:, :], done[:, :], ALU.subtract).then_inc(s_li, 1)
                yield
                dve.wait_ge(s_li, at + 4)
                v.tensor_copy(new[:, :], pre[0][:, E:2 * E])
                for i in range(4):
                    d = 1 << i
                    dve.wait_ge(s_li, at + 4 + i)
                    v.tensor_tensor(pre[1 - i % 2][:, E:2 * E], pre[i % 2][:, E:2 * E], pre[i % 2][:, E - d:2 * E - d],
                                    ALU.add).then_inc(s_li, 1)
                    yield
                S = pre[0][:, E:2 * E]
                dve.wait_ge(s_li, at + 8)
                v.tensor_tensor(sx[:, :], new[:, :], S, ALU.subtract).then_inc(s_li, 1)
                v.tensor_tensor(cmp[:, 0:n, :], bc(cidx[:, 0:n, None], [1, n, E]), bc(S[:, None, :], [1, n, E]), ALU.is_ge)
                v.tensor_scalar(reg[:, E:E + 1], S[:, E - 1:E], -float(P), float(DUMMY), ALU.mult, ALU.add)
                yield
                dve.wait_ge(s_li, at + 9)
                v.tensor_tensor(sx[:, :], sx[:, :], done[:, :], ALU.add).then_inc(s_li, 1)
                yield
                dve.wait_ge(s_li, at + 10)
                v.scalar_tensor_tensor(reg[:, 0:E], sx[:, :], float(P), basef[:, :], ALU.mult, ALU.add).then_inc(s_li, 1)
                v.tensor_reduce(ek[:, 0:n], cmp[:, 0:n, :], X, ALU.add)
                yield
                dve.wait_ge(s_li, at + 11)
                v.tensor_tensor(dreg[:, :], reg[:, 1:E + 1], reg[:, 0:E], ALU.subtract).then_inc(s_li, 1)
                yield
                dve.wait_ge(s_li, at + 12)
                v.tensor_tensor(pr[:, 0:n, :], cmp[:, 0:n, :], bc(dreg[:, None, :], [1, n, E]), ALU.mult).then_inc(s_li, 1)
                yield
                dve.wait_ge(s_li, at + 13)
                v.tensor_reduce(rr[:, 0:n], pr[:, 0:n, :], X, ALU.add).then_inc(s_li, 1)
                yield
                tail = dve.value_load(taili[0:1, 0:1], min_val=0, max_val=TILES)
                v.tensor_scalar(listE[:, bass.ds(tail, n)], ek[:, 0:n], float(E - 1), None, ALU.min)
                v.tensor_copy(done[:, :], full[:, :]).then_inc(s_li, 1)
                v.tensor_tensor(tailf[:, :], tailf[:, :], S[:, E - 1:E], ALU.add).then_inc(s_li, 1)
                dve.wait_ge(s_li, at + 14)
                v.scalar_tensor_tensor(listR[:, bass.ds(tail, n)], rr[:, 0:n], reg[:, 0:1], cidx128[:, 0:n],
                                       ALU.add, ALU.add).then_inc(s_list, 1)
                yield
                dve.wait_ge(s_li, at + 16)
                v.tensor_copy(taili[:, :], tailf[:, :]).then_inc(s_li, 1)
                yield

            def select(s, b, pair):
                u = s * 2 + b
                at = (u * 2 + pair) * KINDS
                wait(dve, s_mask, u + 1)
                wait(dve, s_clr, u + 1)
                wait(dve, s_e, u * GB + 2 * pair + 2)
                into = sel[:, pair * 2 * P:(pair + 1) * 2 * P].rearrange("p (g i) -> p g i", g=2)
                for k in range(KINDS):
                    if k:
                        dve.wait_ge(s_sel, at + k)
                    apart(dve)
                    v.copy_predicated(into, mask[:, k, pair * 2 * P:(pair + 1) * 2 * P].rearrange("p (g i) -> p g i", g=2),
                                      bE[:, :, k * P:(k + 1) * P]).then_inc(s_sel, 1)
                    yield
                if pair == 1:
                    dve.wait_ge(s_sel, at + KINDS)
                    wait(dve, s_tanh, u)
                    v.scalar_tensor_tensor(lk[:, :], sel[:, :], 0.2, sel[:, :], ALU.mult, ALU.max).then_inc(s_lk, 1)
                    yield

            def route(s, b):
                u = s * 2 + b
                at = u * 14
                yield from one_hot_of_max(lg, m1, oh1, at + 1)
                dve.wait_ge(s_rt, at + 6)
                v.scalar_tensor_tensor(lg2[:, :, :], oh1[:, :, :], NEG, lg[:, :, :], ALU.mult, ALU.add).then_inc(s_rt, 1)
                yield
                yield from one_hot_of_max(lg2, m2, oh2, at + 7)
                dve.wait_ge(s_rt, at + 12)
                wait(dve, s_pf, u)
                v.tensor_tensor(dsp[:, :].rearrange("p (g e) -> p g e", g=GB), oh1[:, :, :], oh2[:, :, :], ALU.add).then_inc(s_rt, 1)
                v.tensor_tensor(dlt[:, :], m1[:, :], m2[:, :], ALU.subtract).then_inc(s_rt, 1)
                yield

            def in_turn(chains, steps=1000):
                for _ in range(steps):
                    for chain in list(chains):
                        if next(chain, chain) is chain:
                            chains.remove(chain)

            chains = []

            def body(step, s, b, c):
                u = s * 2 + b
                if step == "MIX":
                    in_turn(chains, c)
                if step == "X1":
                    dve.wait_ge(s_go, u + 1)
                    xu = xall[:, bass.ds(u * (GB * D), GB * D)]
                    v.scalar_tensor_tensor(xu, bT[:, :], 0.5, xu, ALU.mult, ALU.add).then_inc(s_x1, 1)
                if step == "NX" and not (isinstance(s, int) and u < 2):
                    statistics(s, b, 1)
                if step == "NY":
                    statistics(s, b, 0)
                if step == "NB" and parts(s, b)[1] > parts(s, b)[0]:
                    chains.append(norm_b(s, b))
                if step == "RA":
                    chains.append(route(s, b))
                if step == "LG":
                    wait(dve, s_lg, u + 1)
                    wait(dve, s_rt, u * 14)
                    v.tensor_tensor(lg[:, :, :], bR[:, 0:GB * E].rearrange("p (g e) -> p g e", g=GB),
                                    bc(gbr[:, None, :], [P, GB, E]), ALU.add).then_inc(s_rt, 1)
                if step == "CP01":
                    chains.append(select(s, b, 0))
                if step == "CP23":
                    chains.append(select(s, b, 1))
                if step == "LIST":
                    chains.append(append(u, isinstance(s, int) and u == GROUPS - 1))
                if step == "PADS" and isinstance(s, int) and u == GROUPS - 1:
                    dve.wait_ge(s_dummy, 16)
                    v.tensor_copy(padx[:, :, D:D + 1].bitcast(U32), padi2[:, :]).then_inc(s_padi, 1)
                    v.tensor_scalar(pslot[:, :], run[:, :], iop[:, 0:1], None, ALU.add).then_inc(s_padi, 1)
                if step == "MASK":
                    wait(dve, s_adjT, u + 1)
                    for k in range(KINDS):
                        last = v.tensor_single_scalar(mask[:, k, :], adjT[:, :], float(k + 1), ALU.is_equal)
                    last.then_inc(s_mask, 1)
                if step == "SLOT":
                    at = u * 6
                    wait(dve, s_disp[b], s * (2 * GB * 16))
                    v.tensor_copy(hxv[b][:, :, :, D:D + 1].rearrange("p c g r -> p (c g) r").bitcast(U32),
                                  tok[:, bass.ds(u * (2 * GB), 2 * GB)])
                    wait(dve, s_pf, u + 1)
                    v.tensor_tensor(pos[:, :, :], bR[:, GB * E:2 * GB * E].rearrange("p (g e) -> p g e", g=GB),
                                    bc(run[:, None, :], [P, GB, E]), ALU.add).then_inc(s_so, 1)
                    dve.wait_ge(s_so, at + 1)
                    v.tensor_tensor(pm[:, 0, :, :], pos[:, :, :], oh1[:, :, :], ALU.mult).then_inc(s_so, 1)
                    v.tensor_tensor(pm[:, 1, :, :], pos[:, :, :], oh2[:, :, :], ALU.mult).then_inc(s_so, 1)
                    v.tensor_tensor(run[:, :], run[:, :], bR[:, 2 * GB * E:2 * GB * E + E], ALU.add).then_inc(s_so, 1)
                    dve.wait_ge(s_so, at + 3)
                    v.tensor_reduce(slotf[:, :, :], pm[:, :, :, :], X, ALU.add).then_inc(s_so, 1)
                    wait(dve, s_gt, u + 1)
                    v.tensor_scalar(hxv[b][:, 0, :, D + 1], th[:, :], 0.5, 0.5, ALU.mult, ALU.add)
                    v.tensor_scalar(hxv[b][:, 1, :, D + 1], th[:, :], -0.5, 0.5, ALU.mult, ALU.add)
                    dve.wait_ge(s_so, at + 5)
                    v.tensor_copy(slot[b][:, :], slotf[:, :, :].rearrange("p c g -> p (c g)")).then_inc(s_so, 1)
                    dve.wait_ge(s_so, at + 6)
                    apart(dve)
                    dve.sem_inc(s_gate, 1)
                if step == "F":
                    h_ = c - 2
                    if has(s, h_):
                        wait(dve, s_sl, tile(s, h_) + 1)
                        wait(dve, s_tp, tile(s, h_) + 2)
                        v.tensor_tensor(hid[h_ % 2][:, :], sl[h_ % 2][:, :], bH[h_ % 2][:, HID:2 * HID], ALU.mult).then_inc(s_hid, 1)

            for b in range(2):
                statistics(0, b, 1)
                in_turn([norm_b(-1, b)])
            program(dve, body)

            yin = [w12[:, r * 1024:(r + 1) * 1024].rearrange("p (g c d) -> p g c d", g=GB, c=2) for r in range(4)]
            yout = [w3s[:, r * 512:(r + 1) * 512].rearrange("p (g d) -> p g d", g=GB) for r in range(4)]

            def combine(t, r):
                dve.wait_ge(s_yin[r], t * 16 + 16)
                wait(dve, s_out[r], t * 16)
                xv = xall[:, bass.ds(t * (4 * GB * D) + r * GB * D, GB * D)].rearrange("p (g d) -> p g d", g=GB)
                v.tensor_tensor(yout[r], yin[r][:, :, 0, :], yin[r][:, :, 1, :], ALU.add).then_inc(s_a1, 1)
                dve.wait_ge(s_a1, t * 4 + (r + 1))
                v.tensor_tensor(yout[r], yout[r], xv, ALU.add).then_inc(s_a2, 1)

            dve.wait_ge(s_o, TILES)
            for r in range(4):
                combine(0, r)
            with dve.Fori(1, GROUPS // 4) as t:
                for r in range(4):
                    combine(t, r)


_INS = ["x", "adj", "L0_gnn_a0", "L0_gnn_a1", "L0_gnn_a2", "L0_gnn_a3", "L0_gnn_bias", "L0_ffn_gate_w", "L0_ffn_gate_b",
        "L0_ffn_w1", "L0_ffn_w2", "L0_ffn_w3"]


def kernel(**inputs):
    import numpy as _np
    import concourse.bacc as _bacc
    from concourse import mybir as _mybir
    from concourse.bass_utils import run_bass_kernel_spmd as _run

    nc = _bacc.Bacc("TRN2", target_bir_lowering=False, num_devices=1)
    arrays, args = {}, []
    for name in _INS:
        a = _np.ascontiguousarray(inputs[name])
        arrays[f"in_{name}"] = a
        args.append(nc.dram_tensor(f"in_{name}", a.shape, _mybir.dt.from_np(a.dtype), kind="ExternalInput").ap())
    out = nc.dram_tensor("out_x", (G, P, D), _mybir.dt.float32, kind="ExternalOutput").ap()
    build(nc, *args, out)
    r = _run(nc, [arrays], core_ids=[0])
    return r.results[0]["out_x"]
```

```python
from contextlib import ExitStack

import concourse.bass as bass
from concourse import mybir

G, P, D = 128, 128, 128
E, HID = 16, 256
KINDS = 4
GB = 4
GROUPS = G // GB
EPS = 1e-5
NEG = -1.0e30
TOKENS = G * P
CAP = TOKENS + P
FULL_TILES = 2 * TOKENS // P
TILES = FULL_TILES + E - 1
DUMMY = E * CAP
XS_ROWS = DUMMY + E * P
Y_ROWS = 2 * TOKENS + 2 * E * P
ROW = D + 2
TPG = FULL_TILES // GROUPS
LAG = 7
RING = 16
YRING = 8
NEW = TPG + E - 1
LAST = TILES - (TPG * (GROUPS - 1) - (E - 1))
LIST = TILES + LAST
DEPTH = 4

EARLY = 20
COVER = 27
FIRST_SUM = TPG * (COVER + 1) + TPG

ALU = mybir.AluOpType
ACT = mybir.ActivationFunctionType
F32 = mybir.dt.float32
BF16 = mybir.dt.bfloat16
U16 = mybir.dt.uint16
U32 = mybir.dt.uint32
I32 = mybir.dt.int32
X = mybir.AxisListType.X


def build(nc, x, adj, a0, a1, a2, a3, bias, gate_w, gate_b, w1, w2, w3, out):
    xs = nc.dram_tensor("dispatched", [XS_ROWS, ROW], F32, kind="Internal").ap()
    y = nc.dram_tensor("expert_rows", [Y_ROWS, D], F32, kind="Internal").ap()

    with ExitStack() as ctx:
        def sb(name, shape, dt=F32):
            return ctx.enter_context(nc.sbuf_tensor(name, shape, dt))

        def ps(name):
            return ctx.enter_context(nc.psum_tensor(name, [P, 512], F32))

        def sem(name):
            return ctx.enter_context(nc.semaphore(name))

        xall = sb("xall", [P, G * D])
        w12 = sb("w12", [P, E * 2 * HID])
        w3s = sb("w3s", [P, E * 2 * D])
        adji = [sb(f"adji{b}", [P, GB * P], I32) for b in range(2)]
        adjb = sb("adjb", [P, GB * P], BF16)
        st = sb("st", [P, 2 * GB, 6])
        mv = sb("mv", [P, 2 * GB, 2])
        ve = sb("ve", [P, 2 * GB])
        rs = sb("rs", [P, 2 * GB])
        nt = sb("nt", [P, 2 * GB])
        nmr = sb("nmr", [P, 2 * GB])
        hN = [sb(f"hN{b}", [P, GB * D]) for b in range(2)]
        hT = sb("hT", [P, GB * P])
        sc = sb("sc", [P, GB, KINDS, P])
        adjT = sb("adjT", [P, GB * P], BF16)
        mask = sb("mask", [P, KINDS, GB * P], U16)
        sel_lk = sb("sel_lk", [P, 2 * GB * P])
        sel, lk = sel_lk[:, 0:GB * P], sel_lk[:, GB * P:2 * GB * P]
        al_h2T = sb("al_h2T", [P, 2 * GB * P])
        al, h2T = al_h2T[:, 0:GB * P], al_h2T[:, GB * P:2 * GB * P]
        hx = [sb(f"hx{b}", [P, 2 * GB * ROW]) for b in range(2)]
        lg = sb("lg", [P, GB, E])
        lg2 = sb("lg2", [P, GB, E])
        eq = sb("eq", [P, GB, E])
        wq = sb("wq", [P, GB, E])
        oh1 = sb("oh1", [P, GB, E])
        oh2 = sb("oh2", [P, GB, E])
        m1 = sb("m1", [P, GB])
        m2 = sb("m2", [P, GB])
        mx = sb("mx", [P, GB])
        dlt = sb("dlt", [P, GB])
        th = sb("th", [P, GB])
        dsp = sb("dsp", [P, GB * E], BF16)
        pos = sb("pos", [P, GB, E])
        pm = sb("pm", [P, 2, GB, E])
        slotf = sb("slotf", [P, 2, GB])
        slot = [sb(f"slot{b}", [P, 2 * GB], U32) for b in range(2)]
        run = sb("run", [P, E])
        tok = sb("tok", [P, GROUPS * 2 * GB], I32)
        xg = [sb(f"xg{r}", [P, ROW]) for r in range(RING)]
        xh = [sb(f"xh{b}", [P, 3 * P]) for b in range(2)]
        sl = [sb(f"sl{b}", [P, HID]) for b in range(2)]
        hid = [sb(f"hid{b}", [P, HID]) for b in range(2)]
        yo = [sb(f"yo{r}", [P, D]) for r in range(YRING)]
        padx = sb("padx", [P, E, ROW])
        padi = sb("padi", [P, E], I32)
        padi2 = sb("padi2", [P, E], I32)
        pslot = sb("pslot", [P, E], U32)
        basef = sb("basef", [P, E])
        cnti = sb("cnti", [P, E], I32)
        cnth = sb("cnth", [P, E], I32)
        full = sb("full", [P, E])
        done = sb("done", [P, E])
        new = sb("new", [P, E])
        pre = [sb(f"pre{i}", [P, 2 * E]) for i in range(2)]
        sx = sb("sx", [P, E])
        reg = sb("reg", [P, E + 1])
        dreg = sb("dreg", [P, E])
        cmp = sb("cmp", [P, E])
        pr = sb("pr", [P, E])
        ek = sb("ek", [P, 1])
        rr = sb("rr", [P, 1])
        entry = sb("entry", [P, 2])
        ends = sb("ends", [1, GROUPS * E])
        over = sb("over", [1, E])
        early = sb("early", [1, 1], I32)
        earlyf = sb("earlyf", [1, 1])
        listE = sb("listE", [1, LIST], I32)
        listR = sb("listR", [1, LIST], I32)
        tailf = sb("tailf", [1, 1])
        taili = sb("taili", [1, 1], I32)
        ident = sb("ident", [P, P])
        identb = sb("identb", [P, P], BF16)
        tri = sb("tri", [P, P], BF16)
        ones = sb("ones", [P, P], BF16)
        acol = sb("acol", [P, KINDS])
        biasr = sb("biasr", [P, D])
        bres = sb("bres", [P, D])
        bpart = sb("bpart", [P, D], BF16)
        bias3 = sb("bias3", [P, GB * D], BF16)
        gw = sb("gw", [P, E])
        gbr = sb("gbr", [P, E])
        wt = sb("wt", [P, E])
        iop = sb("iop", [P, 1])
        iop128 = sb("iop128", [P, 1])

        bE = ctx.enter_context(nc.psum_tensor("bE", [P, 2, 512], F32))
        bT, bR, bH0, bH1, bXH, bO = [ps(n) for n in ("bT", "bR", "bH0", "bH1", "bXH", "bO")]
        bH = [bH0, bH1]
        adjTp = bR[:, GB * P // 2:GB * P].bitcast(BF16)

        s_x = [sem(f"x_landed{b}") for b in range(2)]
        s_adj = [sem(f"adj_landed{b}") for b in range(2)]
        s_w = sem("weights_landed")
        s_small = sem("small_landed")
        s_c = sem("pool_constants")
        s_cv = sem("dve_constants")
        s_pad0 = sem("pads_built")
        s_dummy = sem("dummy_tiles_stored")
        s_ln = sem("norm_steps")
        s_stat = [sem(f"row_statistics{h}") for h in range(2)]
        s_h = sem("h_written")
        s_adjb = sem("adj_cast")
        s_th = sem("h_transposed")
        s_sc = sem("h_scaled")
        s_adjT = sem("adjT_copied")
        s_mask = sem("masks")
        s_clr = sem("sel_cleared")
        s_e = sem("e_ready")
        s_sel = sem("e_selected")
        s_lk = sem("leaky")
        s_tanh = sem("tanh")
        s_al = sem("alpha")
        s_go = sem("gnn_out")
        s_bias = sem("bias_split_steps")
        s_hx = sem("second_rows_copied")
        s_x1 = sem("x1_written")
        s_h2 = sem("h2_written")
        s_t2 = sem("h2_transposed")
        s_h2T = sem("h2T_copied")
        s_lg = sem("logits")
        s_rt = sem("route_steps")
        s_gt = sem("gate_tanh")
        s_gate = sem("gates_written")
        s_pf = sem("prefix")
        s_so = sem("slot_steps")
        s_li = sem("list_steps")
        s_lrow = sem("list_entries_in_rows")
        s_list = sem("list_appended")
        s_disp = [sem(f"dispatched{b}") for b in range(2)]
        s_padi = sem("pad_slots")
        s_pads = sem("pads_stored")
        s_xg = [sem(f"tile_landed{r}") for r in range(RING)]
        s_tp = sem("tile_transposed")
        s_xh = sem("tile_transposes_copied")
        s_hp = sem("h_products")
        s_sl = sem("silu")
        s_hid = sem("hidden")
        s_o = sem("expert_out")
        s_yo = sem("expert_out_gated")
        s_y = [sem(f"rows_stored{r}") for r in range(YRING)]
        s_apart = sem("waits_taken_apart")
        s_early = sem("early_sums_decided")
        s_yin = [sem(f"y_loaded{r}") for r in range(4)]
        s_a1 = sem("first_sum")
        s_a2 = sem("second_sum")
        s_out = [sem(f"out_stored{r}") for r in range(4)]

        block = ctx.enter_context(nc.Block())

        def wait(eng, s, count):
            if not isinstance(count, int) or count > 0:
                eng.wait_ge(s, count)

        def apart(eng):
            eng.sem_inc(s_apart, 1)

        def bc(ap, shape):
            return ap.to_broadcast(shape)

        ALL = 1000
        ORDER = [("F", 0), ("T1", 0), ("EVA", 0), ("RA", 3), ("NB", 1), ("MIX", 5), ("LIST", 4), ("D3", 4),
                 ("F", 1), ("EVB", 0), ("MIX", 5),
                 ("F", 2), ("EVC", 0), ("MIX", ALL), ("GT", 3),
                 ("F", 3), ("MASK", 0), ("E01", 0), ("H2A", 2), ("H2B", 2), ("LROW", 4), ("PREF", 3),
                 ("F", 4), ("SLOT", 3), ("LISTB", 4), ("CP01", 0), ("MIX", ALL), ("PADS", 4), ("HX", 2), ("T2", 2),
                 ("H2T", 2), ("D0", 3),
                 ("F", 5), ("OUT", 1), ("E23", 0), ("ADJ", -1), ("NX", -2), ("MIX", ALL), ("D1", 3), ("H1A", -1),
                 ("F", 6), ("X1", 1), ("CP23", 0), ("MIX", 3), ("H1B", -1), ("LOG", 2), ("D2", 3),
                 ("F", 7), ("MIX", ALL), ("LG", 2), ("NY", 1), ("TANH", 0), ("LOAD", 0)]
        FIRST_ORDER = [("WARM", 16), ("LIST", 4), ("T1", 0), ("EVA", 0), ("RA", 3), ("NB", 1), ("MIX", 5), ("D3", 4),
                       ("WARM", 12), ("EVB", 0), ("MIX", 5), ("WARM", 12), ("EVC", 0), ("MIX", ALL), ("GT", 3),
                       ("WARM", 20), ("MASK", 0), ("E01", 0), ("H2A", 2), ("H2B", 2), ("LROW", 4), ("PREF", 3), ("SLOT", 3),
                       ("LISTB", 4), ("CP01", 0), ("MIX", ALL), ("PADS", 4), ("HX", 2), ("T2", 2), ("H2T", 2), ("D0", 3),
                       ("WARM", 12), ("OUT", 1), ("E23", 0), ("ADJ", -1), ("NX", -2), ("MIX", ALL), ("D1", 3), ("H1A", -1),
                       ("WARM", 12), ("X1", 1), ("CP23", 0), ("MIX", 3), ("H1B", -1), ("LOG", 2), ("D2", 3), ("WARM", 12),
                       ("MIX", ALL), ("LG", 2), ("NY", 1), ("TANH", 0), ("LOAD", 0)]
        NORMS = ("NB",)
        LAST_S = (TILES - 1 + DEPTH + TPG * LAG) // (2 * TPG)

        def walk(fn, s, first, last):
            for b in range(2):
                for step, back in (FIRST_ORDER if last < (LAG - 1) // 2 else ORDER):
                    if step == "F":
                        c = TPG * (b - LAG) + back
                        if 2 * TPG * last + c >= 0 and 2 * TPG * first + c < TILES + DEPTH:
                            fn("F", s, b, c)
                        continue
                    if step in ("MIX", "WARM"):
                        fn(step, s, b, back)
                        continue
                    at = b - back
                    lo, hi = 2 * first + at, 2 * last + at
                    if hi >= 0 and lo < (GROUPS + 1 if step in NORMS else GROUPS):
                        fn(step, s + at // 2 if at // 2 else s, at % 2, None)

        LOOP = (5, GROUPS // 2 - 2)

        def program(eng, fn):
            for s in range(LOOP[0]):
                walk(fn, s, s, s)
            with eng.Fori(LOOP[0], LOOP[1]) as s:
                walk(fn, s, LOOP[0], LOOP[1] - 1)
            for s in range(LOOP[1], LAST_S + 1):
                walk(fn, s, s, s)

        def has(s, c):
            return not isinstance(s, int) or 0 <= 2 * TPG * s + c < TILES

        def tile(s, c):
            return s * (2 * TPG) + c

        def lap(s, c, ring):
            per = 2 * TPG // ring
            return s * per + (c // ring) + 1

        NORM = 13
        LI = 18
        ROWS = (2 * GB + 1) * E
        scv = sc[:, :, :, :].rearrange("p g k i -> p (g k i)")
        yin = [v_.rearrange("p (g c d) -> p g c d", g=GB, c=2)
               for v_ in (scv[:, 0:1024], scv[:, 1024:2048], sel_lk[:, :], al_h2T[:, :])]
        hxv = [h[:, :].rearrange("p (c g r) -> p c g r", c=2, r=ROW) for h in hx]

        @block.sync
        def _(sp):
            x_g = x.rearrange("g p d -> p g d")
            adj_g = adj.rearrange("g i j -> i g j")

            def load_x(u, b):
                sp.dma_start(xall[:, bass.ds(u * (GB * D), GB * D)].rearrange("p (g d) -> p g d", g=GB),
                             x_g[:, bass.ds(u * GB, GB), :]).then_inc(s_x[b], 16)

            def load_adj(u, b):
                sp.dma_start(adji[b][:, :].rearrange("p (g d) -> p g d", g=GB),
                             adj_g[:, bass.ds(u * GB, GB), :]).then_inc(s_adj[b], 16)

            held = []
            y_g = y[0:2 * TOKENS, :].rearrange("(g p c) d -> p g (c d)", p=P, c=2)

            def load_y(g, r):
                sp.dma_start(yin[r].rearrange("p g c d -> p g (c d)"), y_g[:, bass.ds(g * GB, GB), :]).then_inc(s_yin[r], 16)

            def early_load(q):
                if q == FIRST_SUM:
                    sp.wait_ge(s_e, G)
                    sp.wait_ge(s_tanh, GROUPS)
                    sp.wait_ge(s_go, GROUPS)
                    sp.wait_ge(s_lg, GROUPS)
                    sp.wait_ge(s_early, 4)
                    held.append(sp.value_load(early[0:1, 0:1], min_val=0, max_val=1))
                g, odd = divmod(q - FIRST_SUM, 2)
                if 0 <= g < EARLY and not odd:
                    with sp.If(held[0] == 1):
                        if g == 0:
                            for r in range(YRING):
                                sp.wait_ge(s_y[r], 16 * (TPG * (COVER + 1) // YRING))
                        if g >= 4:
                            sp.wait_ge(s_a2, g - 3)
                        load_y(g, g % 4)

            load_x(0, 0)
            load_adj(0, 0)
            sp.dma_start(acol[:, 0:1], a0).then_inc(s_small, 16)
            sp.dma_start(acol[:, 1:2], a1).then_inc(s_small, 16)
            sp.dma_start(acol[:, 2:3], a2).then_inc(s_small, 16)
            sp.dma_start(acol[:, 3:4], a3).then_inc(s_small, 16)
            sp.dma_start(biasr[:, :], bias.rearrange("(a d) -> a d", a=1).to_broadcast([P, D])).then_inc(s_small, 16)
            sp.dma_start(gbr[:, :], gate_b.rearrange("(a d) -> a d", a=1).to_broadcast([P, E])).then_inc(s_small, 16)
            sp.dma_start(gw[:, :], gate_w).then_inc(s_small, 16)
            load_x(1, 1)
            load_adj(1, 1)
            w12v = w12[:, :].rearrange("p (e w h) -> p e w h", e=E, w=2)
            sp.wait_ge(s_x[0], 16)
            load_x(2, 0)
            sp.dma_start(w12v[:, :, 0, :], w1.rearrange("e d h -> d e h")).then_inc(s_w, 16)
            sp.dma_start(w12v[:, :, 1, :], w2.rearrange("e d h -> d e h")).then_inc(s_w, 16)
            sp.dma_start(w3s[:, :].rearrange("p (e c o) -> p e c o", e=E, c=2),
                         w3.rearrange("e (c p) o -> p e c o", c=2)).then_inc(s_w, 16)
            sp.wait_ge(s_pad0, 1)
            sp.dma_start(xs[DUMMY:DUMMY + E * P, :].rearrange("(e p) r -> p e r", p=P), padx[:, :, :]).then_inc(s_dummy, 16)
            sp.wait_ge(s_dummy, 16)

            def body(step, s, b, c):
                u = s * 2 + b
                if step == "LOAD":
                    if not (isinstance(s, int) and u + 2 >= GROUPS):
                        wait(sp, s_adjb, u + 1)
                        apart(sp)
                        load_adj(u + 2, b)
                    if not (isinstance(s, int) and u + 3 >= GROUPS):
                        wait(sp, s_x[1 - b], (s + b) * 16 + 16)
                        apart(sp)
                        load_x(u + 3, 1 - b)
                if step == "F" and has(s, c):
                    if (c + TPG * LAG) % TPG == 0:
                        if not (isinstance(s, int) and u - 4 > GROUPS):
                            wait(sp, s_list, u - 4)
                            apart(sp)
                            wait(sp, s_disp[1 - b], (s - 2 + b) * (2 * GB * 16))
                        if isinstance(s, int) and u == GROUPS + 4:
                            sp.wait_ge(s_pads, 16 * E)
                    row = sp.value_load(listR[0:1, bass.ds(tile(s, c), 1)], min_val=0, max_val=XS_ROWS - P)
                    wait(sp, s_y[c % YRING], 16 * lap(s, c - RING, YRING))
                    sp.dma_start(xg[c % RING][:, :], xs[bass.ds(row, P), :]).then_inc(s_xg[c % RING], 16)
                if step == "F" and isinstance(s, int):
                    early_load(tile(s, c))

            program(sp, body)

            for r in range(YRING):
                last = max(t for t in range(TILES) if t % YRING == r)
                sp.wait_ge(s_y[r], 16 * (last // YRING + 1))
            with sp.If(held[0] == 0):
                for r in range(4):
                    load_y(r, r)
                with sp.Fori(1, EARLY // 4) as t:
                    for r in range(4):
                        sp.wait_ge(s_a2, t * 4 + (r - 3))
                        load_y(t * 4 + r, r)
            with sp.Fori(EARLY // 4, GROUPS // 4) as t:
                for r in range(4):
                    sp.wait_ge(s_a2, t * 4 + (r - 3))
                    load_y(t * 4 + r, r)

        @block.gpsimd
        def _(pool):
            nc.gpsimd.memset(ident[:, :], 0.0).then_inc(s_c, 1)
            nc.gpsimd.memset(identb[:, :], 0.0).then_inc(s_c, 1)
            nc.gpsimd.memset(tri[:, :], 1.0).then_inc(s_c, 1)
            nc.gpsimd.memset(ones[:, :], 1.0).then_inc(s_c, 1)
            nc.gpsimd.memset(padx[:, :, :], 0.0).then_inc(s_c, 1)
            nc.gpsimd.memset(bias3[:, :], 0.0).then_inc(s_c, 1)
            nc.gpsimd.iota(wt[:, :], pattern=[[-1, E]], base=E, channel_multiplier=0,
                           allow_small_or_imprecise_dtypes=True).then_inc(s_c, 1)
            nc.gpsimd.iota(iop[:, :], pattern=[[0, 1]], base=0, channel_multiplier=1,
                           allow_small_or_imprecise_dtypes=True).then_inc(s_c, 1)
            nc.gpsimd.iota(run[:, :], pattern=[[CAP, E]], base=0, channel_multiplier=0,
                           allow_small_or_imprecise_dtypes=True).then_inc(s_c, 1)
            nc.gpsimd.iota(basef[:, :], pattern=[[CAP, E]], base=0, channel_multiplier=0,
                           allow_small_or_imprecise_dtypes=True).then_inc(s_c, 1)
            nc.gpsimd.iota(iop128[:, :], pattern=[[0, 1]], base=0, channel_multiplier=P,
                           allow_small_or_imprecise_dtypes=True).then_inc(s_c, 1)
            nc.gpsimd.iota(tok[:, :].rearrange("p (u c g) -> p u c g", c=2, g=GB),
                           pattern=[[2 * P * GB, GROUPS], [1, 2], [2 * P, GB]], base=0, channel_multiplier=2).then_inc(s_c, 1)
            nc.gpsimd.iota(padi[:, :], pattern=[[P, E]], base=2 * TOKENS, channel_multiplier=1).then_inc(s_c, 1)
            nc.gpsimd.iota(padi2[:, :], pattern=[[P, E]], base=2 * TOKENS + E * P, channel_multiplier=1).then_inc(s_c, 1)
            pool.wait_ge(s_c, 14)
            nc.gpsimd.affine_select(out=ident[:, :], in_=ident[:, :], compare_op=ALU.not_equal, fill=1.0,
                                    base=0, pattern=[[-1, P]], channel_multiplier=1).then_inc(s_c, 1)
            nc.gpsimd.affine_select(out=identb[:, :], in_=identb[:, :], compare_op=ALU.not_equal, fill=1.0,
                                    base=0, pattern=[[-1, P]], channel_multiplier=1).then_inc(s_c, 1)
            nc.gpsimd.affine_select(out=tri[:, :], in_=tri[:, :], compare_op=ALU.is_gt, fill=0.0,
                                    base=0, pattern=[[1, P]], channel_multiplier=-1).then_inc(s_c, 1)

            def body(step, s, b, c):
                u = s * 2 + b
                if step == "T1":
                    wait(pool, s_lk, u)
                    apart(pool)
                    nc.gpsimd.memset(sel[:, :], NEG).then_inc(s_clr, 1)
                if step in ("D0", "D1", "D2", "D3"):
                    if step == "D0":
                        pool.wait_ge(s_hx, u + 1)
                        pool.wait_ge(s_gate, u + 1)
                        apart(pool)
                    for n in range(2 * int(step[1]), 2 * int(step[1]) + 2):
                        nc.gpsimd.indirect_dma_start(
                            out=xs[:, :], out_offset=bass.IndirectOffsetOnAxis(ap=slot[b][:, n:n + 1], axis=0),
                            in_=hx[b][:, n * ROW:(n + 1) * ROW], in_offset=None).then_inc(s_disp[b], 16)
                if step == "PADS" and isinstance(s, int) and u == GROUPS - 1:
                    pool.wait_ge(s_padi, 2)
                    for e in range(E):
                        nc.gpsimd.indirect_dma_start(
                            out=xs[:, :], out_offset=bass.IndirectOffsetOnAxis(ap=pslot[:, e:e + 1], axis=0),
                            in_=padx[:, e, :], in_offset=None).then_inc(s_pads, 16)
                if step == "F" and has(s, c - DEPTH):
                    o = c - DEPTH
                    wait(pool, s_yo, tile(s, o) + 1)
                    apart(pool)
                    nc.gpsimd.indirect_dma_start(
                        out=y[:, :],
                        out_offset=bass.IndirectOffsetOnAxis(ap=xg[o % RING][:, D:D + 1].bitcast(U32), axis=0),
                        in_=yo[o % YRING][:, :], in_offset=None).then_inc(s_y[o % YRING], 16)

            program(pool, body)

        @block.tensor
        def _(pe):
            pe.wait_ge(s_c, 17)
            pe.wait_ge(s_small, 16 * 7)

            def body(step, s, b, c):
                u = s * 2 + b
                if step == "T1":
                    wait(pe, s_h, u + 1)
                    wait(pe, s_x1, u - 1)
                    for g in range(GB):
                        last = nc.tensor.transpose(bT[:, g * P:(g + 1) * P], hN[b][:, g * D:(g + 1) * D], ident[:, :])
                    last.then_inc(s_th, 1)
                    wait(pe, s_adjb, u + 1)
                    wait(pe, s_adjT, u)
                    wait(pe, s_rt, u * 14 - 41)
                    for g in range(GB):
                        last = nc.tensor.transpose(adjTp[:, g * P:(g + 1) * P], adjb[:, g * P:(g + 1) * P], identb[:, :])
                    last.then_inc(s_th, 1)
                if step in ("E01", "E23"):
                    wait(pe, s_sc, u + 1)
                    pair = 0 if step == "E01" else 1
                    wait(pe, s_sel, (u * 2 + pair) * KINDS)
                    for g in (2 * pair, 2 * pair + 1):
                        nc.tensor.matmul(bE[:, g % 2, :], hT[:, g * P:(g + 1) * P], sc[:, g, :, :].rearrange("p k i -> p (k i)"),
                                         start=True, stop=True).then_inc(s_e, 1)
                if step == "OUT":
                    if isinstance(s, int) and u == 0:
                        pe.wait_ge(s_bias, 8)
                    wait(pe, s_h2T, u)
                    nc.tensor.matmul(bT[:, :], ones[:, :], bias3[:, :], start=True, stop=False, skip_group_check=True)
                    wait(pe, s_al, u + 1)
                    for g in range(GB):
                        last = nc.tensor.matmul(bT[:, g * D:(g + 1) * D], al[:, g * P:(g + 1) * P], hN[b][:, g * D:(g + 1) * D],
                                                start=False, stop=True, skip_group_check=True)
                    last.then_inc(s_go, 1)
                if step == "T2":
                    wait(pe, s_h2, u + 1)
                    wait(pe, s_sc, (u + 3) if not (isinstance(s, int) and u + 2 >= GROUPS) else GROUPS)
                    for g in range(GB):
                        last = nc.tensor.transpose(bT[:, g * P:(g + 1) * P], hxv[b][:, 0, g, 0:D], ident[:, :])
                    last.then_inc(s_t2, 1)
                if step == "LOG":
                    wait(pe, s_h2T, u + 1)
                    wait(pe, s_so, u * 6)
                    wait(pe, s_list, u - 1)
                    for g in range(GB):
                        last = nc.tensor.matmul(bR[:, g * E:(g + 1) * E], h2T[:, g * P:(g + 1) * P], gw[:, :], start=True, stop=True)
                    last.then_inc(s_lg, 1)
                if step == "LROW":
                    wait(pe, s_li, u * LI + 15)
                    wait(pe, s_adjT, (u + 5) if not (isinstance(s, int) and u + 4 >= GROUPS) else GROUPS)
                    n = LAST if isinstance(s, int) and u == GROUPS - 1 else NEW
                    for i in range(2):
                        last = nc.tensor.matmul(bR[0:1, ROWS + i * LAST:ROWS + i * LAST + n], entry[:, i:i + 1], ident[:, 0:n],
                                                start=True, stop=True)
                    last.then_inc(s_lrow, 1)
                if step == "WARM":
                    for n in range(c):
                        nc.tensor.matmul(bH[0][:, 0:P], ones[:, :], identb[:, :], start=True, stop=True)
                if step == "PREF":
                    wait(pe, s_rt, u * 14 + 13)
                    wait(pe, s_adjT, (u + 4) if not (isinstance(s, int) and u + 3 >= GROUPS) else GROUPS)
                    n = GB * E
                    nc.tensor.matmul(bR[:, n:2 * n], tri[:, :], dsp[:, :], start=True, stop=False, skip_group_check=True)
                    for g in range(1, GB):
                        nc.tensor.matmul(bR[:, n + g * E:2 * n], ones[:, :], dsp[:, 0:n - g * E], start=False, stop=(g == GB - 1),
                                         skip_group_check=True)
                    for g in range(GB):
                        last = nc.tensor.matmul(bR[:, 2 * n:2 * n + E], ones[:, :], dsp[:, g * E:(g + 1) * E],
                                                start=False, stop=(g == GB - 1), skip_group_check=True)
                    last.then_inc(s_pf, 1)
                if step == "F":
                    slot_f(s, b, c)

            held = {}

            def expert(s, c):
                if c not in held:
                    held[c] = nc.values_load(listE[0:1, bass.ds(tile(s, c), 1)], engines=[mybir.EngineType.PE],
                                             min_val=0, max_val=E - 1,
                                             skip_runtime_bounds_check_because="the list holds experts only")
                return held[c]

            def slot_f(s, b, c):
                u = s * 2 + b
                x_, h_, t_, o_ = c, c - 1, c - 3, c - DEPTH
                if (c + TPG * LAG) % (2 * TPG) == 0:
                    held.clear()
                if isinstance(s, int) and tile(s, c) == 0:
                    pe.wait_ge(s_w, 48)
                if has(s, x_) or has(s, t_):
                    if (c + TPG * LAG) % TPG == 0 and not (isinstance(s, int) and u - 4 > GROUPS):
                        wait(pe, s_list, u - 4)
                    wait(pe, s_xh, tile(s, c))
                    last = None
                    if has(s, x_):
                        wait(pe, s_xg[x_ % RING], 16 * lap(s, x_, RING))
                        last = nc.tensor.transpose(bXH[:, 0:P], xg[x_ % RING][:, 0:D], ident[:, :])
                    if has(s, t_):
                        wait(pe, s_hid, tile(s, t_) + 1)
                        for h in range(2):
                            last = nc.tensor.transpose(bXH[:, (1 + h) * P:(2 + h) * P], hid[t_ % 2][:, h * P:(h + 1) * P], ident[:, :])
                    last.then_inc(s_tp, 1)
                if has(s, h_):
                    e = expert(s, h_)
                    wait(pe, s_xh, tile(s, h_) + 1)
                    wait(pe, s_hid, tile(s, h_) - 1)
                    nc.tensor.matmul(bH[h_ % 2][:, :], xh[h_ % 2][:, 0:P], w12[:, bass.ds(e * (2 * HID), 2 * HID)],
                                     start=True, stop=True).then_inc(s_hp, 1)
                e = expert(s, o_) if has(s, o_) else None
                if has(s, x_) and (c + TPG * LAG) % (2 * TPG) != 2 * TPG - 1:
                    expert(s, x_)
                if has(s, o_):
                    wait(pe, s_xh, tile(s, c))
                    wait(pe, s_yo, tile(s, o_))
                    for h in range(2):
                        last = nc.tensor.matmul(bO[:, 0:D], xh[(c - 1) % 2][:, (1 + h) * P:(2 + h) * P],
                                                w3s[:, bass.ds(e * (2 * D) + h * D, D)], start=(h == 0), stop=(h == 1))
                    last.then_inc(s_o, 1)

            program(pe, body)

        @block.scalar
        def _(act):

            held = []
            out_g = out.rearrange("g p d -> p g d")

            def store(g, r):
                act.dma_start(out_g[:, bass.ds(g * GB, GB), :],
                              xall[:, bass.ds(g * (GB * D), GB * D)].rearrange("p (g d) -> p g d", g=GB)).then_inc(s_out[r], 16)

            def early_store(q):
                if q == FIRST_SUM:
                    act.wait_ge(s_early, 4)
                    held.append(act.value_load(early[0:1, 0:1], min_val=0, max_val=1))
                g, odd = divmod(q - 4 - FIRST_SUM, 2)
                if 0 <= g < EARLY and not odd:
                    with act.If(held[0] == 1):
                        act.wait_ge(s_a2, g + 1)
                        store(g, g % 4)

            def scaled(k):
                nc.scalar.activation(sc[:, :, k, :], bT[:, :].rearrange("p (g i) -> p g i", g=GB), ACT.Copy,
                                     scale=acol[:, k:k + 1])

            def apply(into, u, g, n):
                return nc.scalar.activation(into, xall[:, bass.ds(u * (GB * D) + g * D, D)], ACT.Identity,
                                            bias=nmr[:, n:n + 1], scale=rs[:, n:n + 1])

            def body(step, s, b, c):
                u = s * 2 + b
                if step == "EVA":
                    wait(act, s_th, u * 2 + 2)
                    wait(act, s_mask, u)
                    nc.scalar.activation(adjT[:, :], adjTp[:, :], ACT.Copy).then_inc(s_adjT, 1)
                    wait(act, s_e, u * GB)
                    scaled(0)
                if step == "EVB":
                    scaled(1)
                    scaled(2)
                if step == "EVC":
                    scaled(3)
                    nc.scalar.activation(hT[:, :], bT[:, :], ACT.Copy).then_inc(s_sc, 1)
                if step in ("H2A", "H2B"):
                    if step == "H2A":
                        act.wait_ge(s_ln, (u + 3) * NORM + NORM)
                        wait(act, s_disp[b], s * (2 * GB * 16))
                    for g in ((0, 1) if step == "H2A" else (2, 3)):
                        last = apply(hxv[b][:, 0, g, 0:D], u, g, g)
                    if step == "H2B":
                        last.then_inc(s_h2, 1)
                if step == "HX":
                    wait(act, s_h2, u + 1)
                    nc.scalar.activation(hxv[b][:, 1, :, 0:D], hxv[b][:, 0, :, 0:D], ACT.Copy).then_inc(s_hx, 1)
                if step in ("H1A", "H1B"):
                    if step == "H1A":
                        wait(act, s_ln, u * NORM + NORM)
                        wait(act, s_go, u - 1)
                    for g in ((0, 1) if step == "H1A" else (2, 3)):
                        last = apply(hN[b][:, g * D:(g + 1) * D], u, g, GB + g)
                    if step == "H1B":
                        last.then_inc(s_h, 1)
                if step == "GT":
                    wait(act, s_rt, u * 14 + 14)
                    wait(act, s_gate, u)
                    nc.scalar.activation(th[:, :], dlt[:, :], ACT.Tanh, scale=0.5).then_inc(s_gt, 1)
                if step == "TANH":
                    wait(act, s_lk, u + 1)
                    wait(act, s_go, u)
                    nc.scalar.activation(al[:, :], lk[:, :], ACT.Tanh, scale=0.5).then_inc(s_tanh, 1)
                    act.wait_ge(s_tanh, u + 1)
                    nc.scalar.activation(al[:, :], al[:, :], ACT.Copy, bias=1.0).then_inc(s_al, 1)
                if step == "ADJ":
                    act.wait_ge(s_adj[b], s * 16 + 16)
                    wait(act, s_th, u * 2)
                    nc.scalar.activation(adjb[:, :], adji[b][:, :], ACT.Copy).then_inc(s_adjb, 1)
                if step == "H2T":
                    wait(act, s_t2, u + 1)
                    wait(act, s_lg, u)
                    nc.scalar.activation(h2T[:, :], bT[:, :], ACT.Copy).then_inc(s_h2T, 1)
                if step == "F":
                    x_, h_, t_, o_ = c, c - 1, c - 3, c - DEPTH
                    if has(s, x_) or has(s, t_):
                        lo = 0 if has(s, x_) else P
                        hi = 3 * P if has(s, t_) else P
                        wait(act, s_tp, tile(s, c) + 1)
                        wait(act, s_hp, tile(s, c) - 1 if has(s, c - 2) else 0)
                        wait(act, s_o, tile(s, c) - 4)
                        nc.scalar.activation(xh[c % 2][:, lo:hi], bXH[:, lo:hi], ACT.Copy).then_inc(s_xh, 1)
                    if has(s, h_):
                        wait(act, s_hp, tile(s, h_) + 1)
                        wait(act, s_hid, tile(s, h_) - 1)
                        nc.scalar.activation(sl[h_ % 2][:, :], bH[h_ % 2][:, 0:HID], ACT.Silu).then_inc(s_sl, 1)
                    if has(s, o_):
                        wait(act, s_o, tile(s, o_) + 1)
                        wait(act, s_y[o_ % YRING], 16 * (lap(s, o_, YRING) - 1))
                        nc.scalar.activation(yo[o_ % YRING][:, :], bO[:, 0:D], ACT.Copy,
                                             scale=xg[o_ % RING][:, D + 1:D + 2]).then_inc(s_yo, 1)
                    if isinstance(s, int):
                        early_store(tile(s, c))

            body("ADJ", 0, 0, None)
            body("H1A", 0, 0, None)
            body("H1B", 0, 0, None)
            act.wait_ge(s_small, 16 * 7)
            program(act, body)

            with act.If(held[0] == 0):
                with act.Fori(0, EARLY // 4) as t:
                    for r in range(4):
                        act.wait_ge(s_a2, t * 4 + (r + 1))
                        store(t * 4 + r, r)
            with act.Fori(EARLY // 4, GROUPS // 4) as t:
                for r in range(4):
                    act.wait_ge(s_a2, t * 4 + (r + 1))
                    store(t * 4 + r, r)
            for r in range(4):
                act.wait_ge(s_out[r], 16 * (GROUPS // 4))

        @block.vector
        def _(dve):
            v = nc.vector
            def parts(s, b):
                u = s * 2 + b
                x1_too = not (isinstance(s, int) and u < 1)
                x_too = not (isinstance(s, int) and u + 2 >= GROUPS)
                return (0 if x1_too else GB), (2 * GB if x_too else GB)

            def statistics(s, b, half):
                u = s * 2 + b
                if half:
                    dve.wait_ge(s_x[b], s * 16 + 16)
                else:
                    dve.wait_ge(s_x1, u + 1)
                apart(dve)
                for g in range(GB):
                    last = v.bn_stats(st[:, half * GB + g, :], rows(u, g))
                    if g == GB - 1:
                        last.then_inc(s_stat[half], 1)
                    yield

            def norm_b(s, b):
                lo, hi = parts(s, b)
                t = s * 2 + b + 2
                at = t * NORM
                if hi > GB:
                    dve.wait_ge(s_stat[1], t + 1)
                if lo == 0:
                    dve.wait_ge(s_stat[0], t - 2)
                wait(dve, s_ln, at)
                apart(dve)
                for g in range(lo, hi):
                    last = v.bn_aggr(mv[:, g, :], st[:, g, :])
                last.then_inc(s_ln, 1)
                yield
                dve.wait_ge(s_ln, at + 1)
                v.tensor_single_scalar(ve[:, lo:hi], mv[:, lo:hi, 1], EPS, ALU.add).then_inc(s_ln, 1)
                yield
                V, R, T = ve[:, lo:hi], rs[:, lo:hi], nt[:, lo:hi]
                dve.wait_ge(s_ln, at + 2)
                wait(dve, s_h, min(t, GROUPS) if isinstance(t, int) else t)
                wait(dve, s_h2, t - 3)
                v.tensor_scalar(R.bitcast(I32), V.bitcast(I32), -0.5, 1597463007.0, ALU.mult, ALU.add).then_inc(s_ln, 1)
                yield
                for i in range(3):
                    dve.wait_ge(s_ln, at + 3 + 3 * i)
                    v.scalar_tensor_tensor(T, R, -0.5, R, ALU.mult, ALU.mult).then_inc(s_ln, 1)
                    yield
                    dve.wait_ge(s_ln, at + 4 + 3 * i)
                    v.tensor_tensor(T, T, V, ALU.mult).then_inc(s_ln, 1)
                    yield
                    dve.wait_ge(s_ln, at + 5 + 3 * i)
                    v.scalar_tensor_tensor(R, T, 1.5, R, ALU.add, ALU.mult).then_inc(s_ln, 1)
                    yield
                dve.wait_ge(s_ln, at + 12)
                v.scalar_tensor_tensor(nmr[:, lo:hi], mv[:, lo:hi, 0], -1.0, R, ALU.mult, ALU.mult).then_inc(s_ln, 1)
                yield

            def rows(u, g):
                return xall[:, bass.ds(u * (GB * D) + g * D, D)]

            def one_hot_of_max(src, m, oh, base):
                dve.wait_ge(s_rt, base)
                v.tensor_reduce(m[:, :], src[:, :, :], X, ALU.max).then_inc(s_rt, 1)
                yield
                dve.wait_ge(s_rt, base + 1)
                v.tensor_tensor(eq[:, :, :], src[:, :, :], bc(m[:, :, None], [P, GB, E]), ALU.is_equal).then_inc(s_rt, 1)
                yield
                dve.wait_ge(s_rt, base + 2)
                v.tensor_tensor(wq[:, :, :], eq[:, :, :], bc(wt[:, None, :], [P, GB, E]), ALU.mult).then_inc(s_rt, 1)
                yield
                dve.wait_ge(s_rt, base + 3)
                v.tensor_reduce(mx[:, :], wq[:, :, :], X, ALU.max).then_inc(s_rt, 1)
                yield
                dve.wait_ge(s_rt, base + 4)
                v.tensor_tensor(oh[:, :, :], wq[:, :, :], bc(mx[:, :, None], [P, GB, E]), ALU.is_equal).then_inc(s_rt, 1)
                yield

            def append(u, final):
                at = u * LI
                wait(dve, s_so, u * 6 + 6)
                wait(dve, s_li, at)
                v.tensor_tensor(cnti[:, :], run[:, :], basef[:, :], ALU.subtract).then_inc(s_li, 1)
                yield
                dve.wait_ge(s_li, at + 1)
                if final:
                    v.tensor_single_scalar(cnti[:, :], cnti[:, :], P - 1, ALU.add).then_inc(s_cv, 1)
                    dve.wait_ge(s_cv, 2)
                v.tensor_single_scalar(cnth[:, :], cnti[:, :], 7, ALU.arith_shift_right).then_inc(s_li, 1)
                yield
                dve.wait_ge(s_li, at + 2)
                v.tensor_copy(full[:, :], cnth[:, :]).then_inc(s_li, 1)
                yield
                dve.wait_ge(s_li, at + 3)
                v.tensor_tensor(pre[0][:, E:2 * E], full[:, :], done[:, :], ALU.subtract).then_inc(s_li, 1)
                yield
                dve.wait_ge(s_li, at + 4)
                v.tensor_copy(new[:, :], pre[0][:, E:2 * E])
                for i in range(4):
                    d = 1 << i
                    dve.wait_ge(s_li, at + 4 + i)
                    v.tensor_tensor(pre[1 - i % 2][:, E:2 * E], pre[i % 2][:, E:2 * E], pre[i % 2][:, E - d:2 * E - d],
                                    ALU.add).then_inc(s_li, 1)
                    yield
                S = pre[0][:, E:2 * E]
                dve.wait_ge(s_li, at + 8)
                v.tensor_tensor(sx[:, :], new[:, :], S, ALU.subtract).then_inc(s_li, 1)
                v.tensor_scalar(cmp[:, :], S, iop[:, 0:1], None, ALU.is_le)
                v.tensor_scalar(reg[:, E:E + 1], S[:, E - 1:E], -float(P), float(DUMMY), ALU.mult, ALU.add)
                yield
                dve.wait_ge(s_li, at + 9)
                v.tensor_tensor(sx[:, :], sx[:, :], done[:, :], ALU.add).then_inc(s_li, 1)
                yield
                dve.wait_ge(s_li, at + 10)
                v.scalar_tensor_tensor(reg[:, 0:E], sx[:, :], float(P), basef[:, :], ALU.mult, ALU.add).then_inc(s_li, 1)
                v.tensor_reduce(ek[:, :], cmp[:, :], X, ALU.add)
                yield
                dve.wait_ge(s_li, at + 11)
                v.tensor_tensor(dreg[:, :], reg[:, 1:E + 1], reg[:, 0:E], ALU.subtract).then_inc(s_li, 1)
                yield
                dve.wait_ge(s_li, at + 12)
                v.tensor_tensor(pr[:, :], cmp[:, :], dreg[:, :], ALU.mult).then_inc(s_li, 1)
                yield
                dve.wait_ge(s_li, at + 13)
                v.tensor_reduce(rr[:, :], pr[:, :], X, ALU.add).then_inc(s_li, 1)
                yield
                dve.wait_ge(s_li, at + 14)
                v.tensor_scalar(entry[:, 0:1], ek[:, :], float(E - 1), None, ALU.min)
                v.scalar_tensor_tensor(entry[:, 1:2], rr[:, :], reg[:, 0:1], iop128[:, :], ALU.add, ALU.add).then_inc(s_li, 1)
                v.tensor_copy(done[:, :], full[:, :]).then_inc(s_li, 1)
                v.tensor_tensor(tailf[:, :], tailf[:, :], pre[0][0:1, 2 * E - 1:2 * E], ALU.add).then_inc(s_li, 1)
                yield

            def append_rows(u, final):
                n = LAST if final else NEW
                tail = dve.value_load(taili[0:1, 0:1], min_val=0, max_val=TILES)
                dve.wait_ge(s_lrow, u + 1)
                v.tensor_copy(listE[:, bass.ds(tail, n)], bR[0:1, ROWS:ROWS + n])
                v.tensor_copy(listR[:, bass.ds(tail, n)], bR[0:1, ROWS + LAST:ROWS + LAST + n]).then_inc(s_list, 1)
                yield
                dve.wait_ge(s_li, u * LI + 17)
                v.tensor_copy(taili[:, :], tailf[:, :]).then_inc(s_li, 1)
                yield

            def select(s, b, pair):
                u = s * 2 + b
                at = (u * 2 + pair) * KINDS
                wait(dve, s_mask, u + 1)
                wait(dve, s_clr, u + 1)
                wait(dve, s_e, u * GB + 2 * pair + 2)
                into = sel[:, pair * 2 * P:(pair + 1) * 2 * P].rearrange("p (g i) -> p g i", g=2)
                for k in range(KINDS):
                    if k:
                        dve.wait_ge(s_sel, at + k)
                    apart(dve)
                    v.copy_predicated(into, mask[:, k, pair * 2 * P:(pair + 1) * 2 * P].rearrange("p (g i) -> p g i", g=2),
                                      bE[:, :, k * P:(k + 1) * P]).then_inc(s_sel, 1)
                    yield
                if pair == 1:
                    dve.wait_ge(s_sel, at + KINDS)
                    wait(dve, s_tanh, u)
                    v.scalar_tensor_tensor(lk[:, :], sel[:, :], 0.2, sel[:, :], ALU.mult, ALU.max).then_inc(s_lk, 1)
                    yield

            def route(s, b):
                u = s * 2 + b
                at = u * 14
                yield from one_hot_of_max(lg, m1, oh1, at + 1)
                dve.wait_ge(s_rt, at + 6)
                v.scalar_tensor_tensor(lg2[:, :, :], oh1[:, :, :], NEG, lg[:, :, :], ALU.mult, ALU.add).then_inc(s_rt, 1)
                yield
                yield from one_hot_of_max(lg2, m2, oh2, at + 7)
                dve.wait_ge(s_rt, at + 12)
                wait(dve, s_pf, u)
                v.tensor_tensor(dsp[:, :].rearrange("p (g e) -> p g e", g=GB), oh1[:, :, :], oh2[:, :, :], ALU.add).then_inc(s_rt, 1)
                v.tensor_tensor(dlt[:, :], m1[:, :], m2[:, :], ALU.subtract).then_inc(s_rt, 1)
                yield

            def places(s, b):
                u = s * 2 + b
                at = u * 6
                wait(dve, s_pf, u + 1)
                v.tensor_tensor(pos[:, :, :], bR[:, GB * E:2 * GB * E].rearrange("p (g e) -> p g e", g=GB),
                                bc(run[:, None, :], [P, GB, E]), ALU.add).then_inc(s_so, 1)
                yield
                wait(dve, s_disp[b], s * (2 * GB * 16))
                v.tensor_copy(hxv[b][:, :, :, D:D + 1].rearrange("p c g r -> p (c g) r").bitcast(U32),
                              tok[:, bass.ds(u * (2 * GB), 2 * GB)])
                dve.wait_ge(s_so, at + 1)
                v.tensor_tensor(pm[:, 0, :, :], pos[:, :, :], oh1[:, :, :], ALU.mult).then_inc(s_so, 1)
                yield
                v.tensor_tensor(pm[:, 1, :, :], pos[:, :, :], oh2[:, :, :], ALU.mult).then_inc(s_so, 1)
                v.tensor_tensor(run[:, :], run[:, :], bR[:, 2 * GB * E:2 * GB * E + E], ALU.add).then_inc(s_so, 1)
                yield
                dve.wait_ge(s_so, at + 4)
                v.tensor_copy(ends[:, bass.ds(u * E, E)], run[0:1, :])
                v.tensor_reduce(slotf[:, :, :], pm[:, :, :, :], X, ALU.add).then_inc(s_so, 1)
                wait(dve, s_gt, u + 1)
                v.tensor_scalar(hxv[b][:, 0, :, D + 1], th[:, :], 0.5, 0.5, ALU.mult, ALU.add)
                v.tensor_scalar(hxv[b][:, 1, :, D + 1], th[:, :], -0.5, 0.5, ALU.mult, ALU.add)
                yield
                dve.wait_ge(s_so, at + 5)
                v.tensor_copy(slot[b][:, :], slotf[:, :, :].rearrange("p c g -> p (c g)")).then_inc(s_so, 1)
                dve.wait_ge(s_so, at + 6)
                apart(dve)
                dve.sem_inc(s_gate, 1)
                yield

            def in_turn(chains, steps=ALL):
                for _ in range(steps):
                    for chain in list(chains):
                        if next(chain, chain) is chain:
                            chains.remove(chain)

            chains = []
            held = []

            def add_rows(g, t, r):
                dve.wait_ge(s_yin[r], t * 16 + 16)
                v.tensor_tensor(yin[r][:, :, 0, :], yin[r][:, :, 0, :], yin[r][:, :, 1, :], ALU.add).then_inc(s_a1, 1)

            def add_x1(g, t, r):
                xv = xall[:, bass.ds(g * (GB * D), GB * D)].rearrange("p (g d) -> p g d", g=GB)
                dve.wait_ge(s_a1, g + 1)
                v.tensor_tensor(xv, xv, yin[r][:, :, 0, :], ALU.add).then_inc(s_a2, 1)

            def early_sum(q):
                if q == FIRST_SUM:
                    held.append(dve.value_load(early[0:1, 0:1], min_val=0, max_val=1))
                g, odd = divmod(q - 3 - FIRST_SUM, 2)
                if 0 <= g < EARLY and not odd:
                    with dve.If(held[0] == 1):
                        add_rows(g, g // 4, g % 4)
                        add_x1(g, g // 4, g % 4)

            def decide(u):
                v.tensor_tensor(over[:, :], ends[:, (EARLY - 1) * E:EARLY * E], basef[0:1, :], ALU.subtract).then_inc(s_early, 1)
                dve.wait_ge(s_early, 1)
                v.scalar_tensor_tensor(over[:, :], done[0:1, :], -float(P), over[:, :], ALU.mult, ALU.add).then_inc(s_early, 1)
                dve.wait_ge(s_early, 2)
                v.tensor_reduce(earlyf[:, :], over[:, :], X, ALU.max).then_inc(s_early, 1)
                dve.wait_ge(s_early, 3)
                v.tensor_single_scalar(early[:, :], earlyf[:, :], 0.0, ALU.is_le).then_inc(s_early, 1)
                dve.wait_ge(s_early, 4)

            def body(step, s, b, c):
                u = s * 2 + b
                if step == "MIX":
                    in_turn(chains, c)
                if step == "X1":
                    dve.wait_ge(s_go, u + 1)
                    xu = xall[:, bass.ds(u * (GB * D), GB * D)]
                    v.scalar_tensor_tensor(xu, bT[:, :], 0.5, xu, ALU.mult, ALU.add).then_inc(s_x1, 1)
                if step == "NX" and not (isinstance(s, int) and u < 2):
                    chains.append(statistics(s, b, 1))
                if step == "NY":
                    in_turn([statistics(s, b, 0)])
                if step == "NB" and parts(s, b)[1] > parts(s, b)[0]:
                    chains.append(norm_b(s, b))
                if step == "RA":
                    chains.append(route(s, b))
                if step == "LG":
                    wait(dve, s_lg, u + 1)
                    wait(dve, s_rt, u * 14)
                    v.tensor_tensor(lg[:, :, :], bR[:, 0:GB * E].rearrange("p (g e) -> p g e", g=GB),
                                    bc(gbr[:, None, :], [P, GB, E]), ALU.add).then_inc(s_rt, 1)
                if step == "CP01":
                    chains.append(select(s, b, 0))
                if step == "CP23":
                    chains.append(select(s, b, 1))
                if step == "LIST":
                    chains.append(append(u, isinstance(s, int) and u == GROUPS - 1))
                if step == "PADS" and isinstance(s, int) and u == COVER:
                    decide(u)
                if step == "LISTB":
                    chains.append(append_rows(u, isinstance(s, int) and u == GROUPS - 1))
                if step == "PADS" and isinstance(s, int) and u == GROUPS - 1:
                    dve.wait_ge(s_dummy, 16)
                    v.tensor_copy(padx[:, :, D:D + 1].bitcast(U32), padi2[:, :]).then_inc(s_padi, 1)
                    v.tensor_scalar(pslot[:, :], run[:, :], iop[:, 0:1], None, ALU.add).then_inc(s_padi, 1)
                if step == "MASK":
                    wait(dve, s_adjT, u + 1)
                    for k in range(KINDS):
                        last = v.tensor_single_scalar(mask[:, k, :], adjT[:, :], float(k + 1), ALU.is_equal)
                    last.then_inc(s_mask, 1)
                if step == "SLOT":
                    chains.append(places(s, b))
                if step == "F":
                    h_ = c - 2
                    if has(s, h_):
                        wait(dve, s_sl, tile(s, h_) + 1)
                        wait(dve, s_tp, tile(s, h_) + 2)
                        v.tensor_tensor(hid[h_ % 2][:, :], sl[h_ % 2][:, :], bH[h_ % 2][:, HID:2 * HID], ALU.mult).then_inc(s_hid, 1)
                    if isinstance(s, int):
                        early_sum(tile(s, c))

            def constants():
                v.memset(done[:, :], 0.0)
                v.memset(pre[0][:, :], 0.0)
                v.memset(pre[1][:, :], 0.0)
                v.memset(tailf[:, :], 0.0)
                v.memset(taili[:, :], 0).then_inc(s_cv, 1)
                yield
                dve.wait_ge(s_c, 17)
                v.tensor_copy(padx[:, :, D:D + 1].bitcast(U32), padi[:, :]).then_inc(s_pad0, 1)
                yield
                dve.wait_ge(s_small, 16 * 7)
                v.tensor_single_scalar(bres[:, :], biasr[:, :], 2.0, ALU.mult).then_inc(s_bias, 1)
                yield
                for i in range(3):
                    dve.wait_ge(s_bias, 3 * i + 1)
                    v.tensor_copy(bpart[:, :], bres[:, :]).then_inc(s_bias, 1)
                    yield
                    dve.wait_ge(s_bias, 3 * i + 2)
                    v.tensor_copy(bias3[32 * i:32 * i + 1, :].rearrange("p (g d) -> p g d", g=GB),
                                  bc(bpart[32 * i:32 * i + 1, None, :], [1, GB, D])).then_inc(s_bias, 1)
                    if i < 2:
                        v.tensor_tensor(bres[:, :], bres[:, :], bpart[:, :], ALU.subtract).then_inc(s_bias, 1)
                        dve.wait_ge(s_bias, 3 * i + 4)
                    yield
                dve.wait_ge(s_cv, 1)
                yield

            in_turn([statistics(0, 0, 1)])
            in_turn([norm_b(-1, 0)])
            in_turn([statistics(0, 1, 1)])
            in_turn([norm_b(-1, 1), constants()])
            program(dve, body)

            with dve.If(held[0] == 0):
                with dve.Fori(0, EARLY // 4) as t:
                    for r in range(4):
                        add_rows(t * 4 + r, t, r)
                        add_x1(t * 4 + r, t, r)
            with dve.Fori(EARLY // 4, GROUPS // 4) as t:
                for r in range(4):
                    add_rows(t * 4 + r, t, r)
                    add_x1(t * 4 + r, t, r)


_INS = ["x", "adj", "L0_gnn_a0", "L0_gnn_a1", "L0_gnn_a2", "L0_gnn_a3", "L0_gnn_bias", "L0_ffn_gate_w", "L0_ffn_gate_b",
        "L0_ffn_w1", "L0_ffn_w2", "L0_ffn_w3"]


def kernel(**inputs):
    import numpy as _np
    import concourse.bacc as _bacc
    from concourse import mybir as _mybir
    from concourse.bass_utils import run_bass_kernel_spmd as _run

    nc = _bacc.Bacc("TRN2", target_bir_lowering=False, num_devices=1)
    arrays, args = {}, []
    for name in _INS:
        a = _np.ascontiguousarray(inputs[name])
        arrays[f"in_{name}"] = a
        args.append(nc.dram_tensor(f"in_{name}", a.shape, _mybir.dt.from_np(a.dtype), kind="ExternalInput").ap())
    out = nc.dram_tensor("out_x", (G, P, D), _mybir.dt.float32, kind="ExternalOutput").ap()
    build(nc, *args, out)
    r = _run(nc, [arrays], core_ids=[0])
    return r.results[0]["out_x"]
```
